# Optimizing a Trainium2 kernel written in Bass

```python
import numpy as np
import jax
import jax.numpy as jnp

def _softmax(x, axis=-1):
    return jax.nn.softmax(x, axis=axis)

def _gelu(x):
    return jax.nn.gelu(x, approximate=True)

def _silu(x):
    return jax.nn.silu(x)

def _sigmoid(x):
    return jax.nn.sigmoid(x)

def _layernorm(x, axis=-1, eps=1e-05):
    m = jnp.mean(x, axis=axis, keepdims=True)
    v = jnp.var(x, axis=axis, keepdims=True)
    return (x - m) / jnp.sqrt(v + eps)

def _scatter_add(tgt, idx, src, axis=0):
    return tgt.at[idx].add(src)

def _segment_sum(src, seg, n):
    return jax.ops.segment_sum(src, seg, n)
kernel_name = 'mk_flamingo_gated_d1_seqx_r4_a44805'

def setup_inputs(seed: int=0):
    np.random.seed(seed)
    _w = jnp.asarray

    def _rec_inputs():
        import jax
        import jax.numpy as jnp
        _rk = jax.random.key(seed)
        x = 7.22e-05 + 1 * jax.random.normal(jax.random.fold_in(_rk, 1), (2, 1024, 256), jnp.float32)
        _lenS = 1024 - jax.random.randint(jax.random.fold_in(_rk, 7), (2,), 0, max(1, 1024 // 4) + 1, jnp.int32)
        _lenS2 = 77 - jax.random.randint(jax.random.fold_in(_rk, 8), (2,), 0, max(1, 77 // 4) + 1, jnp.int32)
        _ctx_1024P = jax.random.normal(jax.random.fold_in(_rk, 11), (2, 16, 256), jnp.float32)
        _ctx_1024c = jax.random.dirichlet(jax.random.fold_in(_rk, 511), 0.3 * jnp.ones((16,), jnp.float32), (2, 77))
        _ctx_1024t = jnp.einsum('bsk,bkd->bsd', _ctx_1024c, _ctx_1024P)
        _ctx_1024t = _ctx_1024t * jax.lax.rsqrt(jnp.mean(jnp.square(_ctx_1024t)) + 1e-12) * 0.953939
        ctx_1024 = 4.13588e-05 + 0.999923 * (_ctx_1024t + 0.3 * jax.random.normal(jax.random.fold_in(_rk, 611), (2, 77, 256), jnp.float32))
        _g = jax.random.normal(jax.random.fold_in(_rk, 9001), (2, 1), jnp.float32)
        _g = jnp.sign(_g) * jnp.maximum(jnp.abs(_g), 1.0) + (_g == 0) * 1.0
        g_xattn = _g[0]
        g_ffn = _g[1]
        return (x, ctx_1024, g_xattn, g_ffn)
    x, ctx_1024, g_xattn, g_ffn = _rec_inputs()

    def _L0_xattn_setup():
        import jax, jax.numpy as jnp
        import numpy as np
        B, S, D = (4, 512, 256)
        KEY_DIM, VALUE_DIM = (256, 256)
        BETA = 1.0 / np.sqrt(D)
        key = jax.random.key(seed)
        ks = jax.random.split(key, 9)
        inv = 1.0 / np.sqrt(D)
        return {'query': jax.random.normal(ks[0], (B, S, D), dtype=jnp.float32), 'key': jax.random.normal(ks[1], (B, S, D), dtype=jnp.float32), 'value': jax.random.normal(ks[2], (B, S, D), dtype=jnp.float32), 'Wq': jax.random.normal(ks[3], (D, KEY_DIM), dtype=jnp.float32) * inv, 'bq': jnp.zeros((KEY_DIM,), dtype=jnp.float32), 'Wk': jax.random.normal(ks[4], (D, KEY_DIM), dtype=jnp.float32) * inv, 'bk': jnp.zeros((KEY_DIM,), dtype=jnp.float32), 'Wv': jax.random.normal(ks[5], (D, VALUE_DIM), dtype=jnp.float32) * inv, 'bv': jnp.zeros((VALUE_DIM,), dtype=jnp.float32)}
    _L0_xattn_all = _L0_xattn_setup()
    _L0_xattn_in = {k: v for k, v in _L0_xattn_all.items() if k in ('Wq', 'bq', 'Wk', 'bk', 'Wv', 'bv')}
    del _L0_xattn_all

    def _L0_ffn_setup():
        import jax, jax.numpy as jnp
        import numpy as np
        E = 8
        K = 2
        D = 256
        H = 4 * D
        EPS = 1e-05
        TEMP = 1.5
        key = jax.random.key(seed)
        ks = jax.random.split(key, 6)
        B, T = (2, 512)
        x = jax.random.normal(ks[0], (B, T, D), dtype=jnp.float32)
        gamma = jnp.ones((D,), dtype=jnp.float32)
        beta = jnp.zeros((D,), dtype=jnp.float32)
        router_w = jax.random.normal(ks[1], (E, D), dtype=jnp.float32) * 0.02
        W1 = jax.random.normal(ks[2], (E, D, H), dtype=jnp.float32) * 0.02
        W2 = jax.random.normal(ks[3], (E, H, D), dtype=jnp.float32) * 0.02
        return {'x': x, 'gamma': gamma, 'beta': beta, 'router_w': router_w, 'W1': W1, 'W2': W2}
    _L0_ffn_all = _L0_ffn_setup()
    _L0_ffn_in = {k: v for k, v in _L0_ffn_all.items() if k in ('gamma', 'beta', 'router_w', 'W1', 'W2')}
    del _L0_ffn_all
    return {'x': x, 'ctx_1024': ctx_1024, 'g_xattn': g_xattn, 'g_ffn': g_ffn, 'L0_xattn_Wq': _L0_xattn_in['Wq'], 'L0_xattn_bq': _L0_xattn_in['bq'], 'L0_xattn_Wk': _L0_xattn_in['Wk'], 'L0_xattn_bk': _L0_xattn_in['bk'], 'L0_xattn_Wv': _L0_xattn_in['Wv'], 'L0_xattn_bv': _L0_xattn_in['bv'], 'L0_ffn_gamma': _L0_ffn_in['gamma'], 'L0_ffn_beta': _L0_ffn_in['beta'], 'L0_ffn_router_w': _L0_ffn_in['router_w'], 'L0_ffn_W1': _L0_ffn_in['W1'], 'L0_ffn_W2': _L0_ffn_in['W2']}

def reference(x, ctx_1024, g_xattn, g_ffn, L0_xattn_Wq, L0_xattn_bq, L0_xattn_Wk, L0_xattn_bk, L0_xattn_Wv, L0_xattn_bv, L0_ffn_gamma, L0_ffn_beta, L0_ffn_router_w, L0_ffn_W1, L0_ffn_W2):
    import jax
    import jax.numpy as jnp

    def _L0_xattn_ref(query, key, value, Wq, bq, Wk, bk, Wv, bv):
        import jax, jax.numpy as jnp
        import numpy as np
        B, S, D = (4, 512, 256)
        KEY_DIM, VALUE_DIM = (256, 256)
        BETA = 1.0 / np.sqrt(D)
        q = query @ Wq + bq
        k = key @ Wk + bk
        v = value @ Wv + bv
        scores = jnp.einsum('bik,bjk->bij', q, k)
        A = jax.nn.softmax(BETA * scores, axis=-1)
        return jnp.einsum('bij,bjk->bik', A, v)

    def _L0_ffn_ref(x, gamma, beta, router_w, W1, W2):
        import jax, jax.numpy as jnp
        import numpy as np
        E = 8
        K = 2
        D = 256
        H = 4 * D
        EPS = 1e-05
        TEMP = 1.5
        res = x
        mu = jnp.mean(x, axis=-1, keepdims=True)
        var = jnp.mean(jnp.square(x - mu), axis=-1, keepdims=True)
        xn = (x - mu) * jax.lax.rsqrt(var + EPS) * gamma + beta
        logits = jnp.einsum('btd,ed->bte', xn, router_w)
        probs = jax.nn.softmax(logits / TEMP, axis=-1)
        w, idx = jax.lax.top_k(probs, K)
        wdense = jnp.sum(jax.nn.one_hot(idx, E, dtype=w.dtype) * w[..., None], axis=-2)
        h = jax.nn.silu(jnp.einsum('btd,edf->betf', xn, W1))
        y = jnp.einsum('betf,efd->betd', h, W2)
        out = jnp.einsum('bte,betd->btd', wdense, y)
        return out + res
    x = x + jnp.tanh(g_xattn[0]) * _L0_xattn_ref(_layernorm(x, axis=-1), ctx_1024, ctx_1024, L0_xattn_Wq, L0_xattn_bq, L0_xattn_Wk, L0_xattn_bk, L0_xattn_Wv, L0_xattn_bv)
    x = x + jnp.tanh(g_ffn[0]) * _L0_ffn_ref(_layernorm(x, axis=-1), L0_ffn_gamma, L0_ffn_beta, L0_ffn_router_w, L0_ffn_W1, L0_ffn_W2)
    return x

_drawn_inputs = setup_inputs


def setup_inputs(seed=0):
    import zlib

    import numpy as np

    out = dict(_drawn_inputs(seed))
    spreads = {'L0_xattn_bq': (0.0, 0.1),
     'L0_xattn_bk': (0.0, 0.1),
     'L0_xattn_bv': (0.0, 0.1),
     'L0_ffn_gamma': (1.0, 0.2),
     'L0_ffn_beta': (0.0, 0.1)}
    factors = {}
    for name, (base, spread) in spreads.items():
        noise = np.random.default_rng([zlib.crc32(name.encode()), seed]).standard_normal(out[name].shape)
        drawn = base * np.exp(spread * noise) if base else spread * noise
        out[name] = jnp.asarray(drawn.astype(out[name].dtype))
    for name, factor in factors.items():
        out[name] = (out[name] * factor).astype(out[name].dtype)
    return out
```

```python
from contextlib import ExitStack

import concourse.bass as bass
from concourse import mybir

ALU = mybir.AluOpType
ACT = mybir.ActivationFunctionType
AX = mybir.AxisListType
F32, F16, BF16, I32 = mybir.dt.float32, mybir.dt.float16, mybir.dt.bfloat16, mybir.dt.int32

P = 128
B, S, D = 2, 1024, 256
C = 77
KD = D // P
NT = B * S // P
G = 4
NG = NT // G
E, H = 8, 1024
HC = H // P
TOP = 2
PAIRS = TOP * NT
TILES = (TOP * B * S + E * (P - 1)) // P
EPS = 1e-5
TEMP = 1.5
BETA = 1.0 / D ** 0.5
W_SCALE, X_SCALE, H_SCALE = 64.0, 16.0, 16.0
CHUNK = KD * H
NW = 2 * E
NSTAGE = 3
TRASH = TOP * B * S


def gated_attention_moe(nc, x, ctx, g_x, g_f, wq, bq, wk, bk, wv, bv, gamma, beta, router, w1, w2, out):
    with ExitStack() as stack:
        def sb(name, shape, dt=F32):
            return stack.enter_context(nc.sbuf_tensor(name, shape, dt))

        def sem(name):
            return stack.enter_context(nc.semaphore(name))

        u_rows = nc.dram_tensor("u_rows", [B * S, D], F32, kind="Internal").ap()
        y_rows = nc.dram_tensor("y_rows", [TRASH + 3 * P, D], F32, kind="Internal").ap()

        ps = stack.enter_context(nc.psum_tensor("ps", [P, 8, 512], F32))

        w_hi = sb("w_hi", [P, NW * CHUNK], F16)
        w_lo = sb("w_lo", [P, NW * CHUNK], F16)
        stage = sb("stage", [P, NSTAGE, CHUNK])
        xs = sb("xs", [P, NT, D])
        arena = sb("arena", [P, 7168])

        def view(start, cols, dt=F32):
            return arena[:, start:start + cols].bitcast(dt) if dt != F32 else arena[:, start:start + cols]

        xn = view(0, G * D).rearrange("p (i d) -> p i d", i=G)
        xT = view(1024, KD * 512).rearrange("p (k t) -> p k t", k=KD)
        uT = view(2048, KD * 512).rearrange("p (k t) -> p k t", k=KD)
        ub = view(3072, 2 * G * D).rearrange("p (n i d) -> p n i d", n=2, i=G)
        pr = view(5120, 2 * G * C).rearrange("p (n i c) -> p n i c", n=2, i=G)
        pT = view(5760, 512)
        cmp = view(6272, 2 * G * E * E).rearrange("p (n i c) -> p n i c", n=2, i=G)
        wq_sb = view(1024, 512).rearrange("p (k n) -> p k n", k=KD)
        wk_sb = view(1536, 512).rearrange("p (k n) -> p k n", k=KD)
        wv_sb = view(2048, 512).rearrange("p (k n) -> p k n", k=KD)
        wqT = view(2560, 512).rearrange("p (m d) -> p m d", m=KD)
        ctx_sb = view(3072, B * D).rearrange("p (b d) -> p b d", b=B)
        ctxT = view(3584, KD * B * C).rearrange("p (k c) -> p k c", k=KD)
        kT = view(3904, KD * B * C).rearrange("p (k c) -> p k c", k=KD)
        rows = view(4224, D)
        at_tile = view(0, PAIRS * TILES // 2, BF16).rearrange("p (k t a) -> p k t a", k=TOP, t=NT)
        coded = view(640, PAIRS * 2 * TILES // 2, BF16).rearrange("p (k t c a) -> p k t c a", k=TOP, t=NT, c=2)
        at_lane = view(1920, PAIRS * P // 2, BF16).rearrange("p (n b) -> p n b", n=PAIRS)
        tot = view(3968, E * NT).rearrange("p (e t) -> p e t", e=E)
        cum = view(4096, E * NT).rearrange("p (e t) -> p e t", e=E)
        pos = view(4224, NT * E).rearrange("p (t e) -> p t e", e=E)
        picked = view(4352, PAIRS * E).rearrange("p (k t e) -> p k t e", k=TOP, t=NT)
        ecmp = view(4608, TILES * E)[0:1].rearrange("p (a e) -> p a e", a=TILES)
        slot = view(4920, 3 * PAIRS).rearrange("p (n c) -> p n c", n=3)
        slot_i = view(5016, 3 * PAIRS, I32).rearrange("p (n c) -> p n c", n=3)
        code = view(5112, 2 * TILES).rearrange("p (n c) -> p n c", n=2)
        dstf = view(5190, 2 * TILES).rearrange("p (n c) -> p n c", n=2)
        etab_f = view(5268, TILES)[0:1]
        ug = view(0, 3 * D).rearrange("p (s d) -> p s d", s=3)
        xf = view(768, D).rearrange("p (k t) -> p k t", k=KD)
        xh = view(1024, 3 * D // 2, F16).rearrange("p (s k t) -> p s k t", s=3, k=KD)
        xl = view(1408, 3 * D // 2, F16).rearrange("p (s k t) -> p s k t", s=3, k=KD)
        hs = view(1792, 3 * 512).rearrange("p (s n) -> p s n", s=3)
        hh = view(3328, 3 * H // 2, F16).rearrange("p (s n) -> p s n", s=3)
        hl = view(4864, 3 * H // 2, F16).rearrange("p (s n) -> p s n", s=3)
        ys = view(6400, 3 * D).rearrange("p (s d) -> p s d", s=3)

        ident = sb("ident", [P, P])
        before = sb("before", [P, P], BF16)
        ones_b = sb("ones_b", [P, P], BF16)
        ones_f = sb("ones_f", [P, P])
        lane_no = sb("lane_no", [P, P], BF16)
        tile_no = sb("tile_no", [P, TILES])
        earlier = sb("earlier", [P, E, E])
        choice_lane = sb("choice_lane", [P, TOP])
        ttile_no = sb("ttile_no", [P, NT])
        trash_row = sb("trash_row", [P, TILES])
        expo = sb("expo", [P, 3 * G])
        bv_sb = sb("bv_sb", [1, D])
        g_sb = sb("g_sb", [1, 2])
        tg = sb("tg", [P, 2])
        cols = sb("cols", [P, KD, 12])
        v_sb = sb("v_sb", [P, B * D])
        gk = sb("gk", [P, KD, B * C])
        s_bias = sb("s_bias", [1, B * C])
        rg = sb("rg", [P, KD, E])
        r_bias = sb("r_bias", [1, E])
        gb16 = sb("gb16", [P, KD, 2])
        stats = sb("stats", [P, G, 6])
        mv = sb("mv", [P, 2, G, 2])
        powin = sb("powin", [P, 2, 3 * G])
        powout = sb("powout", [P, 2, 3 * G])
        small = sb("small", [P, 4, G])
        lg = sb("lg", [P, NT, E])
        rank = sb("rank", [P, G, E])
        sel = sb("sel", [P, TOP, NT, E])
        sel_sum = sb("sel_sum", [P, NT * E], BF16)
        edge = sb("edge", [P, E + 1])
        ecnt = sb("ecnt", [P, 4, E])
        ecnt_i = sb("ecnt_i", [P, 2, E], I32)
        dst = sb("dst", [P, TILES], I32)
        src = sb("src", [P, TILES], I32)
        etab = sb("etab", [1, TILES], I32)
        smx = sb("smx", [P, 2, NT])
        wts = sb("wts", [P, TOP, NT])

        x_in = [sem(f"x_in{g}") for g in range(NG)]
        small_in, w_in = sem("small_in"), [sem(f"w_in{n}") for n in range(NSTAGE)]
        const_made, const_chain = sem("const_made"), sem("const_chain")
        w_hi_made, w_lo_made = sem("w_hi_made"), sem("w_lo_made")
        setup_pe, setup_copied, gates_made = sem("setup_pe"), sem("setup_copied"), sem("gates_made")
        stats1, pow1, xn_made = sem("stats1"), sem("pow1"), sem("xn_made")
        x_turned, xT_made = sem("x_turned"), sem("xT_made")
        scored, centred, exped = sem("scored"), sem("centred"), sem("exped")
        p_turned, pT_made, attended = sem("p_turned"), sem("pT_made"), sem("attended")
        summed, x2_made, stats2, pow2, u_made, res_made = (sem(n) for n in ("summed", "x2_made", "stats2", "pow2", "u_made", "res_made"))
        u_written = [sem(f"u_written{g}") for g in range(NG)]
        u_turned, uT_made = sem("u_turned"), sem("uT_made")
        logits_done, logits_read, ranked = sem("logits_done"), sem("logits_read"), sem("ranked")
        counted, coded_made, coded_out, index_made = (sem(n) for n in ("counted", "coded_made", "coded_out", "index_made"))
        w_centred, w_exped = sem("w_centred"), sem("w_exped")
        dve_step = sem("dve_step")
        gathered = [sem(f"gathered{s}") for s in range(3)]
        scattered = [sem(f"scattered{s}") for s in range(3)]
        uT_ready, xf_made, xh_made, x_ready = sem("uT_ready"), sem("xf_made"), sem("xh_made"), sem("x_ready")
        h_ready, silu_done, hh_made, split_done = sem("h_ready"), sem("silu_done"), sem("hh_made"), sem("split_done")
        y_ready, y_out = sem("y_ready"), sem("y_out")
        y_in = [sem(f"y_in{g}") for g in range(NG)]
        half_done, out_made, out_written = sem("half_done"), sem("out_made"), sem("out_written")

        N_SMALL = 10
        N_CONST = 13

        x_view = x.rearrange("b (p i) d -> b p i d", p=P)
        out_view = out.rearrange("b (p i) d -> b p i d", p=P)
        u_view = u_rows.rearrange("(p t) d -> p t d", p=P)
        y_view = y_rows[0:TRASH].rearrange("(k p t) d -> k p t d", k=TOP, p=P)

        def group(ap, g):
            return ap[g // 2, :, G * (g % 2):G * (g % 2) + G, :]

        def weight_source(n):
            e = n // 2
            if n % 2 == 0:
                return w1[e].rearrange("(k p) n -> p k n", p=P)
            return w2[e].rearrange("(c p) n -> p c n", p=P)

        def tiles_loop(eng, step):
            for j in range(3):
                step(j, j, 0)
            turns = (TILES - 4) // 3
            with eng.Fori(0, turns) as i:
                for t in range(3):
                    step(i * 3 + (3 + t), t, i + 1)
            for j in range(3 * turns + 3, TILES):
                step(j, j % 3, j // 3)

        def y_buf(g, k):
            n = 2 * g + k
            flat = stage[:].rearrange("p s n -> p (s n)")
            ap = flat[:, 1024 * n:1024 * n + 1024] if n < 6 else view(1024 * (n - 6), 1024)
            return ap.rearrange("p (i d) -> p i d", i=G)

        block = stack.enter_context(nc.Block())

        @block.sync
        def _(sp):
            for g in range(NG):
                if g < 2:
                    sp.dma_start(xs[:, G * g:G * g + G, :], group(x_view, g)).then_inc(x_in[g], 16)
                if g == 0:
                    for dst_, src_ in (
                        (ctx_sb[0:C], ctx.rearrange("b c d -> c b d")),
                        (rows[0:1], bq.unsqueeze(0)), (rows[1:2], bk.unsqueeze(0)),
                        (rows[2:3], gamma.unsqueeze(0)), (rows[3:4], beta.unsqueeze(0)),
                        (rows[4:12], router),
                        (wk_sb, wk.rearrange("(k p) n -> p k n", p=P)),
                        (wq_sb, wq.rearrange("(k p) n -> p k n", p=P)),
                        (wv_sb, wv.rearrange("(k p) n -> p k n", p=P)),
                        (bv_sb[:], bv.unsqueeze(0)),
                    ):
                        sp.dma_start(dst_, src_).then_inc(small_in, 16)
            for g in range(2, NG):
                sp.dma_start(xs[:, G * g:G * g + G, :], group(x_view, g)).then_inc(x_in[g], 16)
            for n in range(NW):
                if n >= NSTAGE:
                    sp.wait_ge(w_hi_made, n - NSTAGE + 1)
                    sp.wait_ge(w_lo_made, n - NSTAGE + 1)
                shape = "p (k n) -> p k n"
                sp.dma_start(stage[:, n % NSTAGE].rearrange(shape, k=KD if n % 2 == 0 else HC),
                             weight_source(n)).then_inc(w_in[n % NSTAGE], 16)
            for s in range(3):
                sp.wait_ge(scattered[s], 16 * (TILES // 3))
            for g in range(NG):
                for k in range(TOP):
                    sp.dma_start(y_buf(g, k), y_view[k, :, G * g:G * g + G, :]).then_inc(y_in[g], 16)
            for g in range(NG):
                sp.wait_ge(out_made, g + 1)
                sp.dma_start(group(out_view, g), xs[:, G * g:G * g + G, :]).then_inc(out_written, 16)
            sp.wait_ge(out_written, 16 * NG)

        @block.gpsimd
        def _(pool):
            pool.dma_start(g_sb[:, 0:1], g_x.unsqueeze(0)).then_inc(gates_made, 16)
            pool.dma_start(g_sb[:, 1:2], g_f.unsqueeze(0)).then_inc(gates_made, 16)
            pool.memset(ident[:], 0.0).then_inc(const_chain, 1)
            pool.memset(before[:], 1.0).then_inc(const_chain, 1)
            pool.memset(earlier[:], 1.0).then_inc(const_chain, 1)
            pool.memset(ones_f[:], 1.0).then_inc(const_made, 1)
            pool.memset(ones_b[:], 1.0).then_inc(const_made, 1)
            pool.memset(expo[:, 0:2 * G], -0.5).then_inc(const_made, 1)
            pool.memset(expo[:, 2 * G:3 * G], 0.5).then_inc(const_made, 1)
            pool.memset(edge[:, 0:1], 0.0).then_inc(const_made, 1)
            pool.wait_ge(const_chain, 3)
            pool.affine_select(out=ident[:], in_=ident[:], compare_op=ALU.not_equal, fill=1.0, base=0,
                               pattern=[[-1, P]], channel_multiplier=1).then_inc(const_made, 1)
            pool.affine_select(out=before[:], in_=before[:], compare_op=ALU.is_gt, fill=0.0, base=0,
                               pattern=[[1, P]], channel_multiplier=-1).then_inc(const_made, 1)
            pool.affine_select(out=earlier[:], in_=earlier[:], compare_op=ALU.is_gt, fill=0.0, base=0,
                               pattern=[[1, E], [-1, E]], channel_multiplier=0).then_inc(const_made, 1)

            def numbers(ap, pattern, base, channel):
                pool.iota(ap, pattern=pattern, base=base, channel_multiplier=channel,
                          allow_small_or_imprecise_dtypes=True).then_inc(const_made, 1)

            numbers(lane_no[:], [[1, P]], 0, 0)
            numbers(tile_no[:], [[1, TILES]], 0, 0)
            numbers(choice_lane[:], [[P, TOP]], 1, 1)
            numbers(ttile_no[:], [[1, NT]], 0, 0)
            numbers(trash_row[:].rearrange("p (n r) -> p n r", r=3), [[0, TILES // 3], [P, 3]], TRASH + NT, 1)

            pool.wait_ge(const_made, N_CONST)
            for t in range(NG + 2):
                if t < NG:
                    pool.wait_ge(stats1, t + 1)
                    pool.tensor_tensor(powout[:, 0, 0:G], powin[:, 0, 0:G], expo[:, 0:G], ALU.pow).then_inc(pow1, 1)
                if t >= 2:
                    pool.wait_ge(stats2, t - 1)
                    pool.tensor_tensor(powout[:, 1], powin[:, 1], expo[:], ALU.pow).then_inc(pow2, 1)

            def gather(j):
                pool.indirect_dma_start(out=ug[:, j % 3], out_offset=None, in_=u_rows,
                                        in_offset=bass.IndirectOffsetOnAxis(ap=src[:, j:j + 1], axis=0)
                                        ).then_inc(gathered[j % 3], 16)

            for g in range(NG):
                pool.wait_ge(u_written[g], 16)
            pool.wait_ge(index_made, 1)
            for j in range(3):
                gather(j)
            for j in range(TILES):
                if j + 3 < TILES:
                    pool.wait_ge(uT_ready, j + 1)
                    gather(j + 3)
                pool.wait_ge(y_out, j + 1)
                pool.indirect_dma_start(out=y_rows, out_offset=bass.IndirectOffsetOnAxis(ap=dst[:, j:j + 1], axis=0),
                                        in_=ys[:, j % 3], in_offset=None).then_inc(scattered[j % 3], 16)

        @block.scalar
        def _(act):
            todo = list(range(NW))

            def upper(count):
                for n in todo[:count]:
                    act.wait_ge(w_in[n % NSTAGE], 16 * (n // NSTAGE + 1))
                    act.activation(w_hi[:, n * CHUNK:(n + 1) * CHUNK], stage[:, n % NSTAGE], ACT.Copy,
                                   scale=W_SCALE).then_inc(w_hi_made, 1)
                del todo[:count]

            act.wait_ge(setup_pe, 5)
            act.activation(tg[:], ps[:, 1, 200:202], ACT.Tanh).then_inc(setup_copied, 1)
            for t in range(NG + 2):
                if t < NG:
                    act.wait_ge(x_turned, t + 1)
                    for k in range(KD):
                        act.activation(xT[:, k], ps[:, k], ACT.Copy).then_inc(xT_made, 1)
                upper(1)
                if 1 <= t <= NG:
                    g = t - 1
                    act.wait_ge(centred, g + 1)
                    act.activation(pr[:, g % 2], pr[:, g % 2], ACT.Exp, scale=BETA).then_inc(exped, 1)
                    upper(1)
                    act.wait_ge(p_turned, g + 1)
                    act.activation(pT[0:C], ps[0:C, 3], ACT.Copy).then_inc(pT_made, 1)
                if t >= 2:
                    g = t - 2
                    act.wait_ge(u_made, g + 1)
                    act.dma_start(u_view[:, G * g:G * g + G, :], ub[:, g % 2]).then_inc(u_written[g], 16)
                    act.wait_ge(u_turned, g + 1)
                    for k in range(KD):
                        act.activation(uT[:, k], ps[:, k], ACT.Copy).then_inc(uT_made, 1)
                upper(1)
            upper(NW)
            act.wait_ge(w_centred, 1)
            act.activation(lg[:], lg[:], ACT.Exp, scale=1.0 / TEMP).then_inc(w_exped, 1)

            def step(j, s, turn):
                for half in range(2):
                    act.wait_ge(h_ready, j * 2 + (half + 1))
                    if not isinstance(j, int) or j * 2 + half >= 3:
                        act.wait_ge(split_done, j * 2 + (half - 2))
                    act.activation(hs[:, (2 * s + half) % 3], ps[:, 2 * s + half], ACT.Silu,
                                   scale=1.0 / (W_SCALE * X_SCALE)).then_inc(silu_done, 1)

            tiles_loop(act, step)

        @block.vector
        def _(dve):
            steps = [0]

            def link(ins):
                steps[0] += 1
                ins.then_inc(dve_step, 1)
                dve.wait_ge(dve_step, steps[0])

            todo = list(range(NW))

            def lower(count):
                for n in todo[:count]:
                    dve.wait_ge(w_hi_made, n + 1)
                    dve.scalar_tensor_tensor(out=w_lo[:, n * CHUNK:(n + 1) * CHUNK], in0=stage[:, n % NSTAGE],
                                             scalar=W_SCALE, in1=w_hi[:, n * CHUNK:(n + 1) * CHUNK],
                                             op0=ALU.mult, op1=ALU.subtract).then_inc(w_lo_made, 1)
                del todo[:count]

            def moments(g, which):
                for i in range(G):
                    ins = dve.bn_stats(stats[:, i], xs[:, G * g + i])
                link(ins)
                for i in range(G):
                    ins = dve.bn_aggr(mv[:, which, i], stats[:, i])
                link(ins)

            def setup_copies():
                dve.wait_ge(setup_pe, 1)
                dve.tensor_copy(cols[:].rearrange("p k n -> p (k n)"), ps[:, 7, 0:24]).then_inc(setup_copied, 1)
                dve.tensor_copy(ctxT, ps[:, 6, 0:KD * B * C].rearrange("p (k c) -> p k c", k=KD)).then_inc(setup_copied, 1)
                dve.wait_ge(setup_pe, 2)
                dve.tensor_copy(wqT, ps[:, 4].rearrange("p (m d) -> p m d", m=KD)).then_inc(setup_copied, 1)
                dve.wait_ge(setup_copied, 3)
                for k in range(KD):
                    dve.tensor_scalar(rg[:, k], cols[:, k, 4:12], cols[:, k, 2:3], None, ALU.mult)
                dve.tensor_scalar(gb16[:], cols[:, :, 2:4], X_SCALE, None, ALU.mult)
                dve.wait_ge(setup_pe, 3)
                for m in range(KD):
                    ins = dve.tensor_scalar(kT[:, m], ps[:, 5, m * B * C:(m + 1) * B * C], cols[:, m, 1:2], None, ALU.add)
                ins.then_inc(setup_copied, 1)
                dve.tensor_copy(v_sb[0:C], ps[0:C, 2]).then_inc(setup_copied, 1)
                dve.wait_ge(setup_pe, 4)
                dve.tensor_copy(gk[:], ps[:, 0, 0:KD * B * C].rearrange("p (k c) -> p k c", k=KD)).then_inc(setup_copied, 1)
                dve.wait_ge(setup_pe, 5)
                dve.wait_ge(setup_copied, 7)
                dve.tensor_copy(s_bias[:], ps[0:1, 1, 0:B * C])
                dve.tensor_copy(r_bias[:], ps[0:1, 1, 160:168]).then_inc(setup_copied, 1)

            def norm_x(g):
                dve.wait_ge(x_in[g], 16)
                moments(g, 0)
                dve.tensor_scalar(powin[:, 0, 0:G], mv[:, 0, :, 1], EPS, None, ALU.add).then_inc(stats1, 1)
                if g >= 1:
                    dve.wait_ge(x_turned, g)
                dve.wait_ge(pow1, g + 1)
                for i in range(G):
                    ins = dve.tensor_scalar(xn[:, i], xs[:, G * g + i], mv[:, 0, i, 0:1], powout[:, 0, i:i + 1],
                                            ALU.subtract, ALU.mult)
                ins.then_inc(xn_made, 1)

            def centre(g):
                dve.wait_ge(scored, g + 1)
                scores = ps[:, 2, 0:G * C].rearrange("p (i c) -> p i c", i=G)
                link(dve.tensor_reduce(small[:, 0], scores, AX.X, ALU.max))
                dve.tensor_tensor(pr[:, g % 2], scores, small[:, 0].unsqueeze(2).to_broadcast([P, G, C]),
                                  ALU.subtract).then_inc(centred, 1)

            def residual(g):
                dve.wait_ge(exped, g + 1)
                link(dve.tensor_reduce(small[:, 1], pr[:, g % 2], AX.X, ALU.add))
                link(dve.reciprocal(small[:, 2], small[:, 1]))
                link(dve.tensor_scalar(small[:, 3], small[:, 2], tg[:, 0:1], None, ALU.mult))
                dve.wait_ge(attended, g + 1)
                for i in range(G):
                    row = xs[:, G * g + i]
                    ins = dve.scalar_tensor_tensor(out=row, in0=ps[:, 4 + i // 2, D * (i % 2):D * (i % 2) + D],
                                                   scalar=small[:, 3, i:i + 1], in1=row, op0=ALU.mult, op1=ALU.add)
                ins.then_inc(x2_made, 1)
                dve.wait_ge(x2_made, g + 1)
                moments(g, 1)
                dve.tensor_scalar(powin[:, 1, 0:G], mv[:, 1, :, 1], EPS, None, ALU.add)
                for n in (1, 2):
                    ins = dve.tensor_scalar(powin[:, 1, n * G:(n + 1) * G], mv[:, 1, :, 1], 1.0 + EPS, EPS * EPS,
                                            ALU.mult, ALU.add)
                ins.then_inc(stats2, 1)
                dve.wait_ge(pow2, g + 1)
                link(dve.scalar_tensor_tensor(out=small[:, 0], in0=powout[:, 1, 0:G], scalar=tg[:, 1:2],
                                              in1=powout[:, 1, 2 * G:3 * G], op0=ALU.mult, op1=ALU.mult))
                if g >= 2:
                    dve.wait_ge(u_written[g - 2], 16)
                for i in range(G):
                    ins = dve.tensor_scalar(ub[:, g % 2, i], xs[:, G * g + i], mv[:, 1, i, 0:1],
                                            powout[:, 1, G + i:G + i + 1], ALU.subtract, ALU.mult)
                ins.then_inc(u_made, 1)
                dve.wait_ge(u_made, g + 1)
                for i in range(G):
                    row = xs[:, G * g + i]
                    ins = dve.scalar_tensor_tensor(out=row, in0=ub[:, g % 2, i], scalar=small[:, 0, i:i + 1], in1=row,
                                                   op0=ALU.mult, op1=ALU.add)
                link(ins)

            def rank_experts(g):
                own = lg[:, G * g:G * g + G]
                dve.wait_ge(logits_done, g + 1)
                dve.tensor_copy(own, ps[:, 6, 0:G * E].rearrange("p (i e) -> p i e", i=G)).then_inc(logits_read, 1)
                dve.wait_ge(logits_read, g + 1)
                for i in range(G):
                    l = lg[:, G * g + i]
                    other, mine = l.unsqueeze(1).to_broadcast([P, E, E]), l.unsqueeze(2).to_broadcast([P, E, E])
                    dve.tensor_tensor(cmp[:, 0, i].rearrange("p (e f) -> p e f", e=E), other, mine, ALU.is_gt)
                    ins = dve.tensor_tensor(cmp[:, 1, i].rearrange("p (e f) -> p e f", e=E), other, mine, ALU.is_equal)
                link(ins)
                link(dve.tensor_tensor(cmp[:, 1], cmp[:, 1], earlier[:].rearrange("p e f -> p (e f)").unsqueeze(1).to_broadcast([P, G, E * E]), ALU.mult))
                link(dve.tensor_tensor(cmp[:, 0], cmp[:, 0], cmp[:, 1], ALU.add))
                link(dve.tensor_reduce(rank[:], cmp[:, 0].rearrange("p i (e f) -> p i e f", e=E), AX.X, ALU.add))
                for k in range(TOP):
                    dve.tensor_scalar(sel[:, k, G * g:G * g + G], rank[:], float(k), None, ALU.is_equal)
                dve.tensor_scalar(sel_sum[:, G * E * g:G * E * (g + 1)], rank[:].rearrange("p i e -> p (i e)"),
                                  TOP - 0.5, None, ALU.is_lt).then_inc(ranked, 1)

            dve.wait_ge(const_made, N_CONST)
            for t in range(NG + 3):
                if t < NG:
                    norm_x(t)
                if t == 0:
                    setup_copies()
                lower(1)
                if 2 <= t < NG + 2:
                    residual(t - 2)
                if 1 <= t <= NG:
                    centre(t - 1)
                lower(1)
                if t >= 3:
                    rank_experts(t - 3)
                if t in (1, NG + 1):
                    lower(1)

            for g in (NG - 2, NG - 1):
                dve.wait_ge(u_written[g], 16)
            dve.wait_ge(counted, 1)
            link(dve.tensor_copy(tot, ps[:, 7, NT * E:2 * NT * E].rearrange("p (t e) -> p e t", e=E)))
            flat = "p e t -> p (e t)"
            link(dve.tensor_tensor_scan(cum.rearrange(flat), ones_f[:], tot.rearrange(flat), 0.0, ALU.mult, ALU.add))
            link(dve.tensor_copy(edge[:, 1:E + 1], cum[:, :, NT - 1]))
            link(dve.tensor_tensor(ecnt[:, 0], edge[:, 1:E + 1], edge[:, 0:E], ALU.subtract))
            link(dve.tensor_scalar(ecnt_i[:, 0], ecnt[:, 0], float(P - 1), None, ALU.add))
            link(dve.tensor_scalar(ecnt_i[:, 1], ecnt_i[:, 0], 7, None, ALU.arith_shift_right))
            link(dve.tensor_copy(ecnt[:, 1], ecnt_i[:, 1]))
            link(dve.tensor_tensor_scan(ecnt[:, 2], ones_f[:, 0:E], ecnt[:, 1], 0.0, ALU.mult, ALU.add))
            link(dve.tensor_tensor(ecnt[:, 3], ecnt[:, 2], ecnt[:, 1], ALU.subtract))
            link(dve.scalar_tensor_tensor(out=ecnt[:, 3], in0=ecnt[:, 3], scalar=float(P), in1=edge[:, 0:E],
                                          op0=ALU.mult, op1=ALU.subtract))
            link(dve.tensor_tensor(cum, cum, tot, ALU.subtract))
            link(dve.tensor_tensor(cum, cum, ecnt[:, 3].unsqueeze(2).to_broadcast([P, E, NT]), ALU.add))
            link(dve.tensor_tensor(pos, ps[:, 7, 0:NT * E].rearrange("p (t e) -> p t e", e=E),
                                   cum.rearrange("p e t -> p t e"), ALU.add))
            for k in range(TOP):
                ins = dve.tensor_tensor(picked[:, k], sel[:, k], pos, ALU.mult)
            link(ins)
            link(dve.tensor_reduce(slot[:, 0], picked.rearrange("p k t e -> p (k t) e"), AX.X, ALU.add))
            link(dve.tensor_copy(slot_i[:, 0], slot[:, 0]))
            dve.tensor_scalar(slot_i[:, 1], slot_i[:, 0], 7, None, ALU.arith_shift_right)
            link(dve.tensor_scalar(slot_i[:, 2], slot_i[:, 0], P - 1, None, ALU.bitwise_and))
            link(dve.tensor_copy(slot[:, 1:3], slot_i[:, 1:3]))
            tile_of = slot[:, 1].rearrange("p (k t) -> p k t", k=TOP)
            for k in range(TOP):
                ins = dve.tensor_tensor(at_tile[:, k], tile_no[:].unsqueeze(1).to_broadcast([P, NT, TILES]),
                                        tile_of[:, k].unsqueeze(2).to_broadcast([P, NT, TILES]), ALU.is_equal)
            link(ins)
            for k in range(TOP):
                dve.tensor_scalar(coded[:, k, :, 0], at_tile[:, k], choice_lane[:, k:k + 1], None, ALU.mult)
                dve.tensor_tensor(coded[:, k, :, 1], at_tile[:, k],
                                  ttile_no[:].unsqueeze(2).to_broadcast([P, NT, TILES]), ALU.mult)
            for n in range(PAIRS):
                ins = dve.tensor_scalar(at_lane[:, n], lane_no[:], slot[:, 2, n:n + 1], None, ALU.is_equal)
                if n % 8 == 7:
                    ins.then_inc(coded_made, 1)
            dve.tensor_tensor(ecmp, tile_no[0:1].unsqueeze(2).to_broadcast([1, TILES, E]),
                              ecnt[0:1, 2].unsqueeze(1).to_broadcast([1, TILES, E]), ALU.is_ge).then_inc(dve_step, 1)
            steps[0] += 1
            dve.wait_ge(dve_step, steps[0])
            link(dve.tensor_reduce(etab_f, ecmp, AX.X, ALU.add))
            dve.tensor_scalar(etab[:], etab_f, float(E - 1), float(2 * CHUNK), ALU.min, ALU.mult)
            dve.wait_ge(coded_out, 1)
            link(dve.tensor_copy(code.rearrange("p c a -> p (c a)"), ps[:, 7, 256:256 + 2 * TILES]))
            dve.scalar_tensor_tensor(out=dstf[:, 0], in0=code[:, 0], scalar=0.0, in1=trash_row[:], op0=ALU.is_equal, op1=ALU.mult)
            link(dve.scalar_tensor_tensor(out=dstf[:, 1], in0=code[:, 0], scalar=float(NT), in1=code[:, 1],
                                          op0=ALU.mult, op1=ALU.add))
            link(dve.scalar_tensor_tensor(out=dst[:], in0=dstf[:, 1], scalar=float(-NT), in1=dstf[:, 0],
                                          op0=ALU.add, op1=ALU.add))
            dve.tensor_scalar(src[:], dst[:], B * S - 1, None, ALU.bitwise_and).then_inc(index_made, 1)

            link(dve.tensor_reduce(smx[:, 0], lg[:], AX.X, ALU.max))
            dve.tensor_tensor(lg[:], lg[:], smx[:, 0].unsqueeze(2).to_broadcast([P, NT, E]), ALU.subtract).then_inc(w_centred, 1)
            dve.wait_ge(w_exped, 1)
            link(dve.tensor_reduce(smx[:, 1], lg[:], AX.X, ALU.add))
            link(dve.reciprocal(smx[:, 0], smx[:, 1]))
            link(dve.tensor_scalar(smx[:, 1], smx[:, 0], tg[:, 1:2], 1.0 / (W_SCALE * H_SCALE), ALU.mult, ALU.mult))
            for k in range(TOP):
                ins = dve.tensor_tensor(picked[:, k], sel[:, k], lg[:], ALU.mult)
            link(ins)
            link(dve.tensor_reduce(wts[:].rearrange("p k t -> p (k t)"), picked.rearrange("p k t e -> p (k t) e"), AX.X, ALU.add))
            for k in range(TOP):
                ins = dve.tensor_tensor(wts[:, k], wts[:, k], smx[:, 1], ALU.mult)
            link(ins)

            def prepare(j, s):
                dve.wait_ge(uT_ready, j + 1)
                for k in range(KD):
                    ins = dve.tensor_scalar(xf[:, k], ps[:, 6, k * P:(k + 1) * P], gb16[:, k, 0:1], gb16[:, k, 1:2],
                                            ALU.mult, ALU.add)
                ins.then_inc(xf_made, 1)
                dve.wait_ge(xf_made, j + 1)
                dve.tensor_copy(xh[:, s], xf).then_inc(xh_made, 1)
                dve.wait_ge(xh_made, j + 1)
                dve.tensor_tensor(xl[:, s], xf, xh[:, s], ALU.subtract).then_inc(x_ready, 1)

            def evacuate(j, s, turn):
                dve.wait_ge(y_ready, j + 1)
                if not isinstance(turn, int) or turn > 0:
                    dve.wait_ge(scattered[s], turn * 16)
                dve.tensor_copy(ys[:, s], ps[:, 7, 0:D]).then_inc(y_out, 1)

            def step(j, s, turn):
                if not isinstance(j, int) or j + 1 < TILES:
                    prepare(j + 1, (s + 1) % 3)
                for half in range(2):
                    dve.wait_ge(silu_done, j * 2 + (half + 1))
                    h = hs[:, (2 * s + half) % 3]
                    hi, lo = hh[:, s, 512 * half:512 * half + 512], hl[:, s, 512 * half:512 * half + 512]
                    dve.tensor_scalar(hi, h, H_SCALE, None, ALU.mult).then_inc(hh_made, 1)
                    dve.wait_ge(hh_made, j * 2 + (half + 1))
                    dve.scalar_tensor_tensor(out=lo, in0=h, scalar=H_SCALE, in1=hi, op0=ALU.mult,
                                             op1=ALU.subtract).then_inc(split_done, 1)
                if not isinstance(j, int) or j > 0:
                    evacuate(j - 1, (s + 2) % 3, turn - (s == 0))

            prepare(0, 0)
            tiles_loop(dve, step)
            evacuate(TILES - 1, (TILES - 1) % 3, (TILES - 1) // 3)

            for g in range(NG):
                dve.wait_ge(y_in[g], 16 * TOP)
                for k in range(TOP):
                    for i in range(G):
                        row = xs[:, G * g + i]
                        ins = dve.scalar_tensor_tensor(out=row, in0=y_buf(g, k)[:, i], scalar=wts[:, k, G * g + i:G * g + i + 1],
                                                       in1=row, op0=ALU.mult, op1=ALU.add)
                    if k == 0:
                        ins.then_inc(half_done, 1)
                        dve.wait_ge(half_done, g + 1)
                ins.then_inc(out_made, 1)

        @block.tensor
        def _(pe):
            pe.wait_ge(const_made, N_CONST)
            pe.wait_ge(small_in, 16 * N_SMALL)
            for k in range(KD):
                pe.transpose(ps[:, 7, 12 * k:12 * k + 12], rows[0:12, k * P:(k + 1) * P], ident[0:12, 0:12])
            for k in range(KD):
                for b in range(B):
                    n = (k * B + b) * C
                    ins = pe.transpose(ps[:, 6, n:n + C], ctx_sb[0:C, b, k * P:(k + 1) * P], ident[0:C, 0:C])
            ins.then_inc(setup_pe, 1)
            for m in range(KD):
                for k in range(KD):
                    ins = pe.transpose(ps[:, 4, (m * KD + k) * P:(m * KD + k + 1) * P], wq_sb[:, k, m * P:(m + 1) * P], ident[:])
            ins.then_inc(setup_pe, 1)
            pe.wait_ge(setup_copied, 3)
            for m in range(KD):
                for k in range(KD):
                    pe.matmul(ps[:, 5, m * B * C:(m + 1) * B * C], wk_sb[:, k, m * P:(m + 1) * P], ctxT[:, k],
                              start=(k == 0), stop=(k == KD - 1))
            for b in range(B):
                for k in range(KD):
                    pe.matmul(ps[0:C, 2, b * D:(b + 1) * D], ctxT[:, k, b * C:(b + 1) * C], wv_sb[:, k],
                              start=(k == 0), stop=False)
                ins = pe.matmul(ps[0:C, 2, b * D:(b + 1) * D], ones_f[0:1, 0:C], bv_sb[:], start=False, stop=True)
            ins.then_inc(setup_pe, 1)
            pe.wait_ge(setup_copied, 5)
            for k in range(KD):
                for m in range(KD):
                    ins = pe.matmul(ps[:, 0, k * B * C:(k + 1) * B * C], wqT[:, m, k * P:(k + 1) * P], kT[:, m],
                                    start=(m == 0), stop=(m == KD - 1))
            ins.then_inc(setup_pe, 1)
            for m in range(KD):
                pe.matmul(ps[0:1, 1, 0:B * C], cols[:, m, 0:1], kT[:, m], start=(m == 0), stop=(m == KD - 1))
            for k in range(KD):
                pe.matmul(ps[0:1, 1, 160:168], cols[:, k, 3:4], cols[:, k, 4:12], start=(k == 0), stop=(k == KD - 1))
            pe.wait_ge(gates_made, 32)
            pe.matmul(ps[:, 1, 200:202], ones_f[0:1, :], g_sb[:], start=True, stop=True).then_inc(setup_pe, 1)
            pe.wait_ge(setup_copied, 8)

            for t in range(NG + 2):
                if t < NG:
                    g, b = t, t // 2
                    pe.wait_ge(xn_made, g + 1)
                    if t >= 3:
                        pe.wait_ge(uT_made, KD * (t - 2))
                    for i in range(G):
                        for k in range(KD):
                            ins = pe.transpose(ps[:, k, i * P:(i + 1) * P], xn[:, i, k * P:(k + 1) * P], ident[:])
                    ins.then_inc(x_turned, 1)
                    pe.wait_ge(xT_made, KD * (g + 1))
                    if g >= 1:
                        pe.wait_ge(centred, g)
                    for i in range(G):
                        o = ps[:, 2, i * C:(i + 1) * C]
                        for k in range(KD):
                            pe.matmul(o, xT[:, k, i * P:(i + 1) * P], gk[:, k, b * C:(b + 1) * C], start=(k == 0), stop=False)
                        ins = pe.matmul(o, ones_f[0:1, :], s_bias[:, b * C:(b + 1) * C], start=False, stop=True)
                    ins.then_inc(scored, 1)
                if 1 <= t <= NG:
                    g, b = t - 1, (t - 1) // 2
                    pe.wait_ge(exped, g + 1)
                    for i in range(G):
                        ins = pe.transpose(ps[0:C, 3, i * P:(i + 1) * P], pr[:, g % 2, i], ident[:])
                    ins.then_inc(p_turned, 1)
                    pe.wait_ge(pT_made, g + 1)
                    if g >= 1:
                        pe.wait_ge(x2_made, g)
                    for i in range(G):
                        ins = pe.matmul(ps[:, 4 + i // 2, D * (i % 2):D * (i % 2) + D], pT[0:C, i * P:(i + 1) * P],
                                        v_sb[0:C, b * D:(b + 1) * D], start=True, stop=True)
                    ins.then_inc(attended, 1)
                if t >= 2:
                    g = t - 2
                    pe.wait_ge(u_made, g + 1)
                    for i in range(G):
                        for k in range(KD):
                            ins = pe.transpose(ps[:, k, i * P:(i + 1) * P], ub[:, g % 2, i, k * P:(k + 1) * P], ident[:])
                    ins.then_inc(u_turned, 1)
                    pe.wait_ge(uT_made, KD * (g + 1))
                    if g >= 1:
                        pe.wait_ge(logits_read, g)
                    for i in range(G):
                        o = ps[:, 6, i * E:(i + 1) * E]
                        for k in range(KD):
                            pe.matmul(o, uT[:, k, i * P:(i + 1) * P], rg[:, k], start=(k == 0), stop=False)
                        ins = pe.matmul(o, ones_f[0:1, :], r_bias[:], start=False, stop=True)
                    ins.then_inc(logits_done, 1)

            pe.wait_ge(ranked, NG)
            pe.matmul(ps[:, 7, 0:NT * E], before[:], sel_sum[:], start=True, stop=True)
            pe.matmul(ps[:, 7, NT * E:2 * NT * E], ones_b[:], sel_sum[:], start=True, stop=True).then_inc(counted, 1)
            for n in range(PAIRS):
                if n % 8 == 0:
                    pe.wait_ge(coded_made, n // 8 + 1)
                ins = pe.matmul(ps[:, 7, 256:256 + 2 * TILES], at_lane[:, n],
                                coded[:, n // NT, n % NT].rearrange("p c a -> p (c a)"),
                                start=(n == 0), stop=(n == PAIRS - 1))
            ins.then_inc(coded_out, 1)

            def turn_rows(j, s, turn):
                pe.wait_ge(gathered[s], (turn + 1) * 16)
                if not isinstance(j, int) or j > 0:
                    pe.wait_ge(x_ready, j)
                for k in range(KD):
                    ins = pe.transpose(ps[:, 6, k * P:(k + 1) * P], ug[:, s, k * P:(k + 1) * P], ident[:])
                ins.then_inc(uT_ready, 1)

            def hidden(j, s, at):
                pe.wait_ge(x_ready, j + 1)
                for c in range(HC):
                    o = ps[:, 2 * s + c // 4, (c % 4) * P:(c % 4 + 1) * P]
                    for k in range(KD):
                        cols_ = bass.ds(at + (k * H + c * P), P)
                        pe.matmul(o, w_hi[:, cols_], xh[:, s, k], start=(k == 0), stop=False)
                        pe.matmul(o, w_hi[:, cols_], xl[:, s, k], start=False, stop=False)
                        ins = pe.matmul(o, w_lo[:, cols_], xh[:, s, k], start=False, stop=(k == KD - 1))
                    if c % 4 == 3:
                        ins.then_inc(h_ready, 1)

            def back(j, s, at):
                pe.wait_ge(split_done, j * 2 + 2)
                if not isinstance(j, int) or j > 0:
                    pe.wait_ge(y_out, j)
                o = ps[:, 7, 0:D]
                for c in range(HC):
                    cols_ = bass.ds(at + (CHUNK + c * D), D)
                    hi, lo = hh[:, s, c * P:(c + 1) * P], hl[:, s, c * P:(c + 1) * P]
                    pe.matmul(o, hi, w_hi[:, cols_], start=(c == 0), stop=False)
                    pe.matmul(o, hi, w_lo[:, cols_], start=False, stop=False)
                    ins = pe.matmul(o, lo, w_hi[:, cols_], start=False, stop=(c == HC - 1))
                ins.then_inc(y_ready, 1)

            def place(j):
                return pe.value_load(etab[0:1, bass.ds(j, 1)] if not isinstance(j, int) else etab[0:1, j:j + 1],
                                     min_val=0, max_val=(E - 1) * 2 * CHUNK)

            def step(j, s, turn):
                if not isinstance(j, int) or j + 1 < TILES:
                    turn_rows(j + 1, (s + 1) % 3, turn + (s == 2))
                hidden(j, s, place(j))
                if not isinstance(j, int) or j > 0:
                    back(j - 1, (s + 2) % 3, place(j - 1))

            pe.wait_ge(index_made, 1)
            pe.wait_ge(w_lo_made, NW)
            turn_rows(0, 0, 0)
            tiles_loop(pe, step)
            back(TILES - 1, (TILES - 1) % 3, place(TILES - 1))


_INS = ["x", "ctx_1024", "g_xattn", "g_ffn", "L0_xattn_Wq", "L0_xattn_bq", "L0_xattn_Wk", "L0_xattn_bk",
        "L0_xattn_Wv", "L0_xattn_bv", "L0_ffn_gamma", "L0_ffn_beta", "L0_ffn_router_w", "L0_ffn_W1", "L0_ffn_W2"]


def kernel(**inputs):
    import numpy as _np
    import concourse.bacc as _bacc
    from concourse import mybir as _mybir
    from concourse.bass_utils import run_bass_kernel_spmd as _run

    nc = _bacc.Bacc("TRN2", target_bir_lowering=False, num_devices=1)
    arrays, args = {}, []
    for name in _INS:
        a = _np.ascontiguousarray(inputs[name])
        arrays[f"in_{name}"] = a
        args.append(nc.dram_tensor(f"in_{name}", a.shape, _mybir.dt.from_np(a.dtype), kind="ExternalInput").ap())
    out = nc.dram_tensor("out_0", (B, S, D), F32, kind="ExternalOutput").ap()
    gated_attention_moe(nc, *args, out)
    r = _run(nc, [arrays], core_ids=[0])
    return r.results[0]["out_0"]
```

```python
from contextlib import ExitStack

import concourse.bass as bass
from concourse import mybir

ALU = mybir.AluOpType
ACT = mybir.ActivationFunctionType
AX = mybir.AxisListType
F32, F16, BF16, I32 = mybir.dt.float32, mybir.dt.float16, mybir.dt.bfloat16, mybir.dt.int32

P = 128
B, S, D = 2, 1024, 256
C = 77
KD = D // P
NT = B * S // P
G = 4
NG = NT // G
E, H = 8, 1024
HC = H // P
TOP = 2
PAIRS = TOP * NT
TILES = (TOP * B * S + E * (P - 1)) // P
EPS = 1e-5
TEMP = 1.5
BETA = 1.0 / D ** 0.5
ACT_FILL = [[0, 1], [2, 3], [4, 5], [6], [7, 8], [9]]
DVE_FILL = [([], [0]), ([1], [2]), ([3], []), ([4], [5]), ([6], []), ([7], [8]), ([9], [])]
W_SCALE, X_SCALE, H_SCALE = 64.0, 16.0, 16.0
CHUNK = KD * H
NW = 2 * E
NSTAGE = 3
EARLY = 10
PEELED = 3
TRASH = TOP * B * S


def gated_attention_moe(nc, x, ctx, g_x, g_f, wq, bq, wk, bk, wv, bv, gamma, beta, router, w1, w2, out):
    with ExitStack() as stack:
        def sb(name, shape, dt=F32):
            return stack.enter_context(nc.sbuf_tensor(name, shape, dt))

        def sem(name):
            return stack.enter_context(nc.semaphore(name))

        u_rows = nc.dram_tensor("u_rows", [B * S, D], F32, kind="Internal").ap()
        y_rows = nc.dram_tensor("y_rows", [TRASH + 3 * P, D], F32, kind="Internal").ap()

        ps = stack.enter_context(nc.psum_tensor("ps", [P, 8, 512], F32))

        w_hi = sb("w_hi", [P, NW * CHUNK], F16)
        w_lo = sb("w_lo", [P, NW * CHUNK], F16)
        stage = sb("stage", [P, NSTAGE, CHUNK])
        xs = sb("xs", [P, NT, D])
        arena = sb("arena", [P, 7168])

        def view(start, cols, dt=F32):
            return arena[:, start:start + cols].bitcast(dt) if dt != F32 else arena[:, start:start + cols]

        xn = view(0, G * D).rearrange("p (i d) -> p i d", i=G)
        xT = view(1024, KD * 512).rearrange("p (k t) -> p k t", k=KD)
        uT = view(2048, KD * 512).rearrange("p (k t) -> p k t", k=KD)
        ub = view(3072, 2 * G * D).rearrange("p (n i d) -> p n i d", n=2, i=G)
        pr = view(5120, 2 * G * C).rearrange("p (n i c) -> p n i c", n=2, i=G)
        pT = view(5760, 512)
        late_hi = w_hi[:, (NW - 2) * CHUNK:].bitcast(F32)
        late_lo = w_lo[:, (NW - 2) * CHUNK:].bitcast(F32)
        wq_sb = late_lo[:, 0:512].rearrange("p (k n) -> p k n", k=KD)
        wk_sb = late_lo[:, 512:1024].rearrange("p (k n) -> p k n", k=KD)
        wv_sb = late_lo[:, 1024:1536].rearrange("p (k n) -> p k n", k=KD)
        wqT = late_lo[:, 1536:2048].rearrange("p (m d) -> p m d", m=KD)
        ctx_sb = late_hi[:, 0:512].rearrange("p (b d) -> p b d", b=B)
        rows = late_hi[:, 512:768]
        ctxT = late_hi[:, 768:768 + KD * B * C].rearrange("p (k c) -> p k c", k=KD)
        kT = late_hi[:, 1088:1088 + KD * B * C].rearrange("p (k c) -> p k c", k=KD)
        at_tile = view(0, PAIRS * TILES // 2, BF16).rearrange("p (k t a) -> p k t a", k=TOP, t=NT)
        coded = view(640, PAIRS * 2 * TILES // 2, BF16).rearrange("p (k t c a) -> p k t c a", k=TOP, t=NT, c=2)
        at_lane = view(1920, PAIRS * P // 2, BF16).rearrange("p (n b) -> p n b", n=PAIRS)
        tot = view(3968, E * NT).rearrange("p (e t) -> p e t", e=E)
        cum = view(4096, E * NT).rearrange("p (e t) -> p e t", e=E)
        pos = view(4224, NT * E).rearrange("p (t e) -> p t e", e=E)
        picked = view(4352, PAIRS * E).rearrange("p (k t e) -> p k t e", k=TOP, t=NT)
        ecmp = view(4608, TILES * E)[0:1].rearrange("p (a e) -> p a e", a=TILES)
        slot = view(4920, 3 * PAIRS).rearrange("p (n c) -> p n c", n=3)
        slot_i = view(5016, 3 * PAIRS, I32).rearrange("p (n c) -> p n c", n=3)
        code = view(5112, 2 * TILES).rearrange("p (n c) -> p n c", n=2)
        dstf = view(5190, 2 * TILES).rearrange("p (n c) -> p n c", n=2)
        etab_f = view(5268, TILES)[0:1]
        ug = view(0, 3 * D).rearrange("p (s d) -> p s d", s=3)
        xf = view(768, D).rearrange("p (k t) -> p k t", k=KD)
        xh = view(1024, 3 * D // 2, F16).rearrange("p (s k t) -> p s k t", s=3, k=KD)
        xl = view(1408, 3 * D // 2, F16).rearrange("p (s k t) -> p s k t", s=3, k=KD)
        hs = view(1792, H)
        hh = view(2816, H // 2, F16)
        hl = view(3328, H // 2, F16)
        ys = view(3840, 3 * D).rearrange("p (s d) -> p s d", s=3)

        ident = sb("ident", [P, P])
        before = sb("before", [P, P], BF16)
        ones_b = sb("ones_b", [P, P], BF16)
        ones_f = sb("ones_f", [P, P])
        lane_no = sb("lane_no", [P, P], BF16)
        tile_no = sb("tile_no", [P, TILES])
        choice_lane = sb("choice_lane", [P, TOP])
        expert_no = sb("expert_no", [P, G, E])
        ttile_no = sb("ttile_no", [P, NT])
        trash_row = sb("trash_row", [P, TILES])
        expo = sb("expo", [P, 3 * G])
        bv_sb = sb("bv_sb", [1, D])
        g_sb = sb("g_sb", [1, 2])
        tg = sb("tg", [P, 2])
        cols = sb("cols", [P, KD, 12])
        v_sb = sb("v_sb", [P, B * D])
        gk = sb("gk", [P, KD, B * C])
        s_bias = sb("s_bias", [1, B * C])
        rg = sb("rg", [P, KD, E])
        r_bias = sb("r_bias", [1, E])
        gb16 = sb("gb16", [P, KD, 2])
        stats = sb("stats", [P, G, 6])
        mv = sb("mv", [P, 2, 2, G, 2])
        powin = sb("powin", [P, 3, 3 * G])
        powout = sb("powout", [P, 3, 3 * G])
        small = sb("small", [P, 5, G])
        lg = sb("lg", [P, G, E])
        top = sb("top", [P, NT, E])
        top_no = sb("top_no", [P, NT, E], mybir.dt.uint32)
        sel = sb("sel", [P, TOP, NT, E])
        sel_sum = sb("sel_sum", [P, NT * E], BF16)
        edge = sb("edge", [P, E + 1])
        ecnt = sb("ecnt", [P, 4, E])
        ecnt_i = sb("ecnt_i", [P, 2, E], I32)
        dst = sb("dst", [P, TILES], I32)
        src = sb("src", [P, TILES], I32)
        etab = sb("etab", [1, TILES], I32)
        smx = sb("smx", [P, 2, NT])
        wts = sb("wts", [P, TOP, NT])

        x_in = [sem(f"x_in{g}") for g in range(NG)]
        small_in, w_in = sem("small_in"), [sem(f"w_in{n}") for n in range(NSTAGE)]
        const_made, const_chain = sem("const_made"), sem("const_chain")
        w_hi_made, w_lo_made = sem("w_hi_made"), sem("w_lo_made")
        setup_pe, setup_copied, gates_in = sem("setup_pe"), sem("setup_copied"), sem("gates_in")
        ident_made, gates_made = sem("ident_made"), sem("gates_made")
        stats1, pow1, xn_made = sem("stats1"), sem("pow1"), sem("xn_made")
        x_turned, xT_made = sem("x_turned"), sem("xT_made")
        scored, centred, exped = sem("scored"), sem("centred"), sem("exped")
        p_turned, pT_made, attended = sem("p_turned"), sem("pT_made"), sem("attended")
        summed, x2_made, stats2, pow2, u_made, res_made = (sem(n) for n in ("summed", "x2_made", "stats2", "pow2", "u_made", "res_made"))
        u_written = [sem(f"u_written{g}") for g in range(NG)]
        u_turned, uT_made = sem("u_turned"), sem("uT_made")
        logits_done, logits_read, ranked = sem("logits_done"), sem("logits_read"), sem("ranked")
        counted, coded_made, coded_out, index_made = (sem(n) for n in ("counted", "coded_made", "coded_out", "index_made"))
        w_centred, w_exped = sem("w_centred"), sem("w_exped")
        dve_step = sem("dve_step")
        gathered = [sem(f"gathered{s}") for s in range(3)]
        scattered = [sem(f"scattered{s}") for s in range(3)]
        uT_ready, xf_made, xh_made, x_ready = sem("uT_ready"), sem("xf_made"), sem("xh_made"), sem("x_ready")
        h_ready, silu_done, hT_ready = sem("h_ready"), sem("silu_done"), sem("hT_ready")
        hh_made, split_done = sem("hh_made"), sem("split_done")
        y_ready, y_out = sem("y_ready"), sem("y_out")
        y_in = [sem(f"y_in{g}") for g in range(NG)]
        half_done, out_made, out_written = sem("half_done"), sem("out_made"), sem("out_written")

        N_SMALL = 10
        N_CONST = 12

        x_view = x.rearrange("b (p i) d -> b p i d", p=P)
        out_view = out.rearrange("b (p i) d -> b p i d", p=P)
        u_view = u_rows.rearrange("(p t) d -> p t d", p=P)
        y_view = y_rows[0:TRASH].rearrange("(k p t) d -> k p t d", k=TOP, p=P)

        def group(ap, g):
            return ap[g // 2, :, G * (g % 2):G * (g % 2) + G, :]

        def weight_source(n):
            e = n // 2
            if n % 2 == 0:
                return w1[e].rearrange("(k p) n -> p k n", p=P)
            return w2[e].rearrange("(c p) n -> p c n", p=P)

        def tiles_loop(eng, step):
            for j in range(PEELED):
                step(j, j, 0)
            with eng.Fori(0, (TILES - PEELED) // 3) as i:
                for t in range(3):
                    step(i * 3 + (3 + t), t, i + 1)

        def late(j):
            first = EARLY + 2 * j
            return range(first, min(first + 2, NW)) if isinstance(j, int) else range(0)

        def y_buf(g, k):
            n = 2 * g + k
            flat = stage[:].rearrange("p s n -> p (s n)")
            ap = flat[:, 1024 * n:1024 * n + 1024] if n < 6 else view(1024 * (n - 6), 1024)
            return ap.rearrange("p (i d) -> p i d", i=G)

        block = stack.enter_context(nc.Block())

        @block.sync
        def _(sp):
            def load_x(g):
                sp.dma_start(xs[:, G * g:G * g + G, :], group(x_view, g)).then_inc(x_in[g], 16)

            def load_small(dst_, src_):
                sp.dma_start(dst_, src_).then_inc(small_in, 16)

            load_x(0)
            load_small(ctx_sb[0:C], ctx.rearrange("b c d -> c b d"))
            load_small(rows[0:1], bq.unsqueeze(0))
            load_small(rows[1:2], bk.unsqueeze(0))
            load_small(rows[2:3], gamma.unsqueeze(0))
            load_small(rows[3:4], beta.unsqueeze(0))
            load_small(rows[4:12], router)
            load_x(1)
            for w_sb, w in ((wq_sb, wq), (wk_sb, wk), (wv_sb, wv)):
                load_small(w_sb, w.rearrange("(k p) n -> p k n", p=P))
            load_small(bv_sb[:], bv.unsqueeze(0))
            for g in range(2, NG):
                load_x(g)
            for n in range(NW):
                if n >= NSTAGE:
                    sp.wait_ge(w_hi_made, n - NSTAGE + 1)
                    sp.wait_ge(w_lo_made, n - NSTAGE + 1)
                shape = "p (k n) -> p k n"
                sp.dma_start(stage[:, n % NSTAGE].rearrange(shape, k=KD if n % 2 == 0 else HC),
                             weight_source(n)).then_inc(w_in[n % NSTAGE], 16)
            for s in range(3):
                sp.wait_ge(scattered[s], 16 * (TILES // 3))
            for g in range(NG):
                for k in range(TOP):
                    sp.dma_start(y_buf(g, k), y_view[k, :, G * g:G * g + G, :]).then_inc(y_in[g], 16)
            for g in range(NG):
                sp.wait_ge(out_made, g + 1)
                sp.dma_start(group(out_view, g), xs[:, G * g:G * g + G, :]).then_inc(out_written, 16)
            sp.wait_ge(out_written, 16 * NG)

        @block.gpsimd
        def _(pool):
            pool.memset(ident[:], 0.0).then_inc(const_chain, 1)
            pool.wait_ge(const_chain, 1)
            pool.affine_select(out=ident[:], in_=ident[:], compare_op=ALU.not_equal, fill=1.0, base=0,
                               pattern=[[-1, P]], channel_multiplier=1).then_inc(ident_made, 1)
            pool.memset(expo[:, 0:2 * G], -0.5).then_inc(const_made, 1)
            pool.memset(expo[:, 2 * G:3 * G], 0.5).then_inc(const_made, 1)
            pool.wait_ge(const_made, 2)

            def power_x(g):
                pool.wait_ge(stats1, g + 1)
                pool.tensor_tensor(powout[:, g % 2, 0:G], powin[:, g % 2, 0:G], expo[:, 0:G], ALU.pow).then_inc(pow1, 1)

            def power_x2(g):
                pool.wait_ge(stats2, g + 1)
                pool.tensor_tensor(powout[:, 2], powin[:, 2], expo[:], ALU.pow).then_inc(pow2, 1)

            power_x(0)
            pool.memset(ones_f[:], 1.0).then_inc(const_made, 1)
            pool.dma_start(g_sb[:, 0:1], g_x.unsqueeze(0)).then_inc(gates_in, 16)
            pool.dma_start(g_sb[:, 1:2], g_f.unsqueeze(0)).then_inc(gates_in, 16)
            power_x(1)
            pool.memset(ones_b[:], 1.0).then_inc(const_made, 1)
            pool.memset(edge[:, 0:1], 0.0).then_inc(const_made, 1)
            pool.memset(before[:], 1.0).then_inc(const_chain, 1)
            pool.wait_ge(const_chain, 2)
            pool.affine_select(out=before[:], in_=before[:], compare_op=ALU.is_gt, fill=0.0, base=0,
                               pattern=[[1, P]], channel_multiplier=-1).then_inc(const_made, 1)

            def numbers(ap, pattern, base, channel):
                pool.iota(ap, pattern=pattern, base=base, channel_multiplier=channel,
                          allow_small_or_imprecise_dtypes=True).then_inc(const_made, 1)

            numbers(lane_no[:], [[1, P]], 0, 0)
            numbers(tile_no[:], [[1, TILES]], 0, 0)
            numbers(choice_lane[:], [[P, TOP]], 1, 1)
            numbers(ttile_no[:], [[1, NT]], 0, 0)
            numbers(expert_no[:], [[0, G], [1, E]], 0, 0)
            numbers(trash_row[:].rearrange("p (n r) -> p n r", r=3), [[0, TILES // 3], [P, 3]], TRASH + NT, 1)
            power_x(2)
            for t in range(2, NG + 2):
                power_x2(t - 2)
                if t + 1 < NG:
                    power_x(t + 1)

            def gather(j):
                col = min(j, TILES - 1)
                pool.indirect_dma_start(out=ug[:, j % 3], out_offset=None, in_=u_rows,
                                        in_offset=bass.IndirectOffsetOnAxis(ap=src[:, col:col + 1], axis=0)
                                        ).then_inc(gathered[j % 3], 16)

            for g in range(NG):
                pool.wait_ge(u_written[g], 16)
            pool.wait_ge(index_made, 1)
            for j in range(3):
                gather(j)
            for j in range(TILES):
                if j + 3 <= TILES:
                    pool.wait_ge(uT_ready, j + 1)
                    gather(j + 3)
                pool.wait_ge(y_out, j + 1)
                pool.indirect_dma_start(out=y_rows, out_offset=bass.IndirectOffsetOnAxis(ap=dst[:, j:j + 1], axis=0),
                                        in_=ys[:, j % 3], in_offset=None).then_inc(scattered[j % 3], 16)

        @block.scalar
        def _(act):
            def upper(n):
                act.wait_ge(w_in[n % NSTAGE], 16 * (n // NSTAGE + 1))
                act.activation(w_hi[:, n * CHUNK:(n + 1) * CHUNK], stage[:, n % NSTAGE], ACT.Copy,
                               scale=W_SCALE).then_inc(w_hi_made, 1)

            def copy(to, of):
                act.activation(to, of, ACT.Copy).then_inc(setup_copied, 1)

            def turned_x(g):
                act.wait_ge(x_turned, g + 1)
                for k in range(KD):
                    act.activation(xT[:, k], ps[:, k], ACT.Copy).then_inc(xT_made, 1)

            act.wait_ge(setup_pe, 1)
            copy(cols[:].rearrange("p k n -> p (k n)"), ps[:, 7, 0:24])
            copy(ctxT, ps[:, 6, 0:KD * B * C].rearrange("p (k c) -> p k c", k=KD))
            act.wait_ge(setup_pe, 2)
            copy(wqT, ps[:, 4].rearrange("p (m d) -> p m d", m=KD))
            act.wait_ge(setup_pe, 3)
            act.wait_ge(setup_copied, 1)
            for m in range(KD):
                act.activation(kT[:, m], ps[:, 5, m * B * C:(m + 1) * B * C], ACT.Identity,
                               bias=cols[:, m, 1:2]).then_inc(setup_copied, 1)
            turned_x(0)
            for k in range(KD):
                act.activation(rg[:, k], cols[:, k, 4:12], ACT.Copy, scale=cols[:, k, 2:3]).then_inc(setup_copied, 1)
            act.activation(gb16[:], cols[:, :, 2:4], ACT.Copy, scale=X_SCALE).then_inc(setup_copied, 1)
            act.wait_ge(setup_pe, 4)
            copy(gk[:], ps[:, 4, 0:KD * B * C].rearrange("p (k c) -> p k c", k=KD))
            act.wait_ge(setup_pe, 5)
            copy(s_bias[:], ps[0:1, 7, 32:32 + B * C])
            copy(r_bias[:], ps[0:1, 7, 200:208])
            copy(v_sb[0:C], ps[0:C, 3])
            act.activation(tg[:], ps[:, 7, 210:212], ACT.Tanh).then_inc(gates_made, 1)

            for n in ACT_FILL[0]:
                upper(n)
            for t in range(1, NG + 2):
                if 1 <= t <= NG:
                    g = t - 1
                    act.wait_ge(centred, g + 1)
                    act.activation(pr[:, g % 2], pr[:, g % 2], ACT.Exp, scale=BETA).then_inc(exped, 1)
                    act.wait_ge(p_turned, g + 1)
                    act.activation(pT[0:C], ps[0:C, 3], ACT.Copy).then_inc(pT_made, 1)
                if t >= 2:
                    g = t - 2
                    act.wait_ge(u_made, g + 1)
                    act.dma_start(u_view[:, G * g:G * g + G, :], ub[:, g % 2]).then_inc(u_written[g], 16)
                    act.wait_ge(u_turned, g + 1)
                    for k in range(KD):
                        act.activation(uT[:, k], ps[:, k], ACT.Copy).then_inc(uT_made, 1)
                if t < NG:
                    turned_x(t)
                for n in ACT_FILL[t]:
                    upper(n)
            act.wait_ge(w_centred, 1)
            act.activation(top[:], top[:], ACT.Exp, scale=1.0 / TEMP).then_inc(w_exped, 1)

            def upper_hidden(j):
                for half in range(2):
                    part = slice(512 * half, 512 * half + 512)
                    act.wait_ge(hT_ready, j * 2 + (half + 1))
                    act.activation(hh[:, part], ps[:, 2 + half], ACT.Copy, scale=H_SCALE).then_inc(hh_made, 1)

            def step(j, s, turn):
                if not isinstance(j, int) or j > 0:
                    upper_hidden(j - 1)
                for half in range(2):
                    act.wait_ge(h_ready, j * 2 + (half + 1))
                    act.activation(hs[:, 512 * half:512 * half + 512], ps[:, half], ACT.Silu,
                                   scale=1.0 / (W_SCALE * X_SCALE)).then_inc(silu_done, 1)
                for n in late(j):
                    upper(n)

            tiles_loop(act, step)
            upper_hidden(TILES - 1)

        @block.vector
        def _(dve):
            steps = [0]

            def link(ins):
                steps[0] += 1
                ins.then_inc(dve_step, 1)
                dve.wait_ge(dve_step, steps[0])

            def lower(n):
                dve.wait_ge(w_hi_made, n + 1)
                dve.scalar_tensor_tensor(out=w_lo[:, n * CHUNK:(n + 1) * CHUNK], in0=stage[:, n % NSTAGE],
                                         scalar=W_SCALE, in1=w_hi[:, n * CHUNK:(n + 1) * CHUNK],
                                         op0=ALU.mult, op1=ALU.subtract).then_inc(w_lo_made, 1)

            def moments(g, which):
                for i in range(G):
                    ins = dve.bn_stats(stats[:, i], xs[:, G * g + i])
                link(ins)
                for i in range(G):
                    ins = dve.bn_aggr(mv[:, which, g % 2, i], stats[:, i])
                link(ins)

            def variance_x(g):
                dve.wait_ge(x_in[g], 16)
                moments(g, 0)
                dve.tensor_scalar(powin[:, g % 2, 0:G], mv[:, 0, g % 2, :, 1], EPS, None, ALU.add).then_inc(stats1, 1)

            def norm_x(g):
                if g >= 1:
                    dve.wait_ge(x_turned, g)
                dve.wait_ge(pow1, g + 1)
                for i in range(G):
                    ins = dve.tensor_scalar(xn[:, i], xs[:, G * g + i], mv[:, 0, g % 2, i, 0:1],
                                            powout[:, g % 2, i:i + 1], ALU.subtract, ALU.mult)
                ins.then_inc(xn_made, 1)

            def centre(g):
                dve.wait_ge(scored, g + 1)
                scores = ps[:, 2, 0:G * C].rearrange("p (i c) -> p i c", i=G)
                link(dve.tensor_reduce(small[:, 0], scores, AX.X, ALU.max))
                dve.tensor_tensor(pr[:, g % 2], scores, small[:, 0].unsqueeze(2).to_broadcast([P, G, C]),
                                  ALU.subtract).then_inc(centred, 1)

            def attend(g):
                dve.wait_ge(exped, g + 1)
                link(dve.tensor_reduce(small[:, 1], pr[:, g % 2], AX.X, ALU.add))
                link(dve.reciprocal(small[:, 2], small[:, 1]))
                if g == 0:
                    dve.wait_ge(gates_made, 1)
                link(dve.tensor_scalar(small[:, 3], small[:, 2], tg[:, 0:1], None, ALU.mult))
                dve.wait_ge(attended, g + 1)
                for i in range(G):
                    row = xs[:, G * g + i]
                    ins = dve.scalar_tensor_tensor(out=row, in0=ps[:, 4 + i // 2, D * (i % 2):D * (i % 2) + D],
                                                   scalar=small[:, 3, i:i + 1], in1=row, op0=ALU.mult, op1=ALU.add)
                ins.then_inc(x2_made, 1)
                dve.wait_ge(x2_made, g + 1)
                moments(g, 1)
                var = mv[:, 1, g % 2, :, 1]
                dve.tensor_scalar(powin[:, 2, 0:G], var, EPS, None, ALU.add)
                for n in (1, 2):
                    ins = dve.tensor_scalar(powin[:, 2, n * G:(n + 1) * G], var, 1.0 + EPS, EPS * EPS, ALU.mult, ALU.add)
                ins.then_inc(stats2, 1)

            def norm_x2(g):
                dve.wait_ge(pow2, g + 1)
                if g >= 2:
                    dve.wait_ge(u_written[g - 2], 16)
                for i in range(G):
                    ins = dve.tensor_scalar(ub[:, g % 2, i], xs[:, G * g + i], mv[:, 1, g % 2, i, 0:1],
                                            powout[:, 2, G + i:G + i + 1], ALU.subtract, ALU.mult)
                ins.then_inc(u_made, 1)
                link(dve.scalar_tensor_tensor(out=small[:, 4], in0=powout[:, 2, 0:G], scalar=tg[:, 1:2],
                                              in1=powout[:, 2, 2 * G:3 * G], op0=ALU.mult, op1=ALU.mult))
                for i in range(G):
                    row = xs[:, G * g + i]
                    ins = dve.scalar_tensor_tensor(out=row, in0=ub[:, g % 2, i], scalar=small[:, 4, i:i + 1], in1=row,
                                                   op0=ALU.mult, op1=ALU.add)
                link(ins)

            def choose(g):
                own = slice(G * g, G * g + G)
                dve.wait_ge(logits_done, g + 1)
                dve.tensor_copy(lg[:], ps[:, 6, 0:G * E].rearrange("p (i e) -> p i e", i=G)).then_inc(logits_read, 1)
                dve.wait_ge(logits_read, g + 1)
                for i in range(G):
                    ins = dve.max(top[:, G * g + i], lg[:, i])
                link(ins)
                for i in range(G):
                    ins = dve.max_index(top_no[:, G * g + i], top[:, G * g + i], lg[:, i])
                link(ins)
                for k in range(TOP):
                    ins = dve.tensor_tensor(sel[:, k, own], expert_no[:],
                                            top_no[:, own, k:k + 1].to_broadcast([P, G, E]), ALU.is_equal)
                link(ins)
                dve.tensor_tensor(sel_sum[:, G * E * g:G * E * (g + 1)].rearrange("p (i e) -> p i e", i=G),
                                  sel[:, 0, own], sel[:, 1, own], ALU.add).then_inc(ranked, 1)

            variance_x(0)
            for t in range(NG + 3):
                if 2 <= t < NG + 2:
                    attend(t - 2)
                if t + 1 < NG:
                    variance_x(t + 1)
                if 1 <= t <= NG:
                    centre(t - 1)
                for n in DVE_FILL[t][0]:
                    lower(n)
                if 2 <= t < NG + 2:
                    norm_x2(t - 2)
                if t < NG:
                    norm_x(t)
                for n in DVE_FILL[t][1]:
                    lower(n)
                if t == 3:
                    dve.wait_ge(const_made, N_CONST)
                if t >= 3:
                    choose(t - 3)

            for g in (NG - 2, NG - 1):
                dve.wait_ge(u_written[g], 16)
            dve.wait_ge(counted, 1)
            link(dve.tensor_copy(tot, ps[:, 7, NT * E:2 * NT * E].rearrange("p (t e) -> p e t", e=E)))
            flat = "p e t -> p (e t)"
            link(dve.tensor_tensor_scan(cum.rearrange(flat), ones_f[:], tot.rearrange(flat), 0.0, ALU.mult, ALU.add))
            link(dve.tensor_copy(edge[:, 1:E + 1], cum[:, :, NT - 1]))
            link(dve.tensor_tensor(ecnt[:, 0], edge[:, 1:E + 1], edge[:, 0:E], ALU.subtract))
            link(dve.tensor_scalar(ecnt_i[:, 0], ecnt[:, 0], float(P - 1), None, ALU.add))
            link(dve.tensor_scalar(ecnt_i[:, 1], ecnt_i[:, 0], 7, None, ALU.arith_shift_right))
            link(dve.tensor_scalar(ecnt[:, 1], ecnt_i[:, 1], 1.0, None, ALU.max))
            link(dve.tensor_tensor_scan(ecnt[:, 2], ones_f[:, 0:E], ecnt[:, 1], 0.0, ALU.mult, ALU.add))
            link(dve.tensor_tensor(ecnt[:, 3], ecnt[:, 2], ecnt[:, 1], ALU.subtract))
            link(dve.scalar_tensor_tensor(out=ecnt[:, 3], in0=ecnt[:, 3], scalar=float(P), in1=edge[:, 0:E],
                                          op0=ALU.mult, op1=ALU.subtract))
            link(dve.tensor_tensor(cum, cum, tot, ALU.subtract))
            link(dve.tensor_tensor(cum, cum, ecnt[:, 3].unsqueeze(2).to_broadcast([P, E, NT]), ALU.add))
            link(dve.tensor_tensor(pos, ps[:, 7, 0:NT * E].rearrange("p (t e) -> p t e", e=E),
                                   cum.rearrange("p e t -> p t e"), ALU.add))
            for k in range(TOP):
                ins = dve.tensor_tensor(picked[:, k], sel[:, k], pos, ALU.mult)
            link(ins)
            link(dve.tensor_reduce(slot[:, 0], picked.rearrange("p k t e -> p (k t) e"), AX.X, ALU.add))
            link(dve.tensor_copy(slot_i[:, 0], slot[:, 0]))
            dve.tensor_scalar(slot_i[:, 1], slot_i[:, 0], 7, None, ALU.arith_shift_right)
            link(dve.tensor_scalar(slot_i[:, 2], slot_i[:, 0], P - 1, None, ALU.bitwise_and))
            link(dve.tensor_copy(slot[:, 1:3], slot_i[:, 1:3]))
            tile_of = slot[:, 1].rearrange("p (k t) -> p k t", k=TOP)
            for k in range(TOP):
                ins = dve.tensor_tensor(at_tile[:, k], tile_no[:].unsqueeze(1).to_broadcast([P, NT, TILES]),
                                        tile_of[:, k].unsqueeze(2).to_broadcast([P, NT, TILES]), ALU.is_equal)
            link(ins)
            for k in range(TOP):
                dve.tensor_scalar(coded[:, k, :, 0], at_tile[:, k], choice_lane[:, k:k + 1], None, ALU.mult)
                dve.tensor_tensor(coded[:, k, :, 1], at_tile[:, k],
                                  ttile_no[:].unsqueeze(2).to_broadcast([P, NT, TILES]), ALU.mult)
            for n in range(PAIRS):
                ins = dve.tensor_scalar(at_lane[:, n], lane_no[:], slot[:, 2, n:n + 1], None, ALU.is_equal)
                if n % 8 == 7:
                    ins.then_inc(coded_made, 1)
            dve.tensor_tensor(ecmp, tile_no[0:1].unsqueeze(2).to_broadcast([1, TILES, E]),
                              ecnt[0:1, 2].unsqueeze(1).to_broadcast([1, TILES, E]), ALU.is_ge).then_inc(dve_step, 1)
            steps[0] += 1
            dve.wait_ge(dve_step, steps[0])
            link(dve.tensor_reduce(etab_f, ecmp, AX.X, ALU.add))
            dve.tensor_scalar(etab[:], etab_f, float(E - 1), float(2 * CHUNK), ALU.min, ALU.mult)
            dve.wait_ge(coded_out, 1)
            link(dve.tensor_copy(code.rearrange("p c a -> p (c a)"), ps[:, 7, 256:256 + 2 * TILES]))
            dve.scalar_tensor_tensor(out=dstf[:, 0], in0=code[:, 0], scalar=0.0, in1=trash_row[:], op0=ALU.is_equal, op1=ALU.mult)
            link(dve.scalar_tensor_tensor(out=dstf[:, 1], in0=code[:, 0], scalar=float(NT), in1=code[:, 1],
                                          op0=ALU.mult, op1=ALU.add))
            link(dve.scalar_tensor_tensor(out=dst[:], in0=dstf[:, 1], scalar=float(-NT), in1=dstf[:, 0],
                                          op0=ALU.add, op1=ALU.add))
            dve.tensor_scalar(src[:], dst[:], B * S - 1, None, ALU.bitwise_and).then_inc(index_made, 1)

            link(dve.tensor_copy(smx[:, 0], top[:, :, 0]))
            dve.tensor_tensor(top[:], top[:], smx[:, 0].unsqueeze(2).to_broadcast([P, NT, E]), ALU.subtract).then_inc(w_centred, 1)
            dve.wait_ge(w_exped, 1)
            link(dve.tensor_reduce(smx[:, 1], top[:], AX.X, ALU.add))
            link(dve.reciprocal(smx[:, 0], smx[:, 1]))
            link(dve.tensor_scalar(smx[:, 1], smx[:, 0], tg[:, 1:2], 1.0 / (W_SCALE * H_SCALE), ALU.mult, ALU.mult))
            for k in range(TOP):
                ins = dve.tensor_tensor(wts[:, k], top[:, :, k], smx[:, 1], ALU.mult)
            link(ins)

            def prepare(j, s):
                dve.wait_ge(uT_ready, j + 1)
                for k in range(KD):
                    ins = dve.tensor_scalar(xf[:, k], ps[:, 6, k * P:(k + 1) * P], gb16[:, k, 0:1], gb16[:, k, 1:2],
                                            ALU.mult, ALU.add)
                ins.then_inc(xf_made, 1)
                dve.wait_ge(xf_made, j + 1)
                dve.tensor_copy(xh[:, s], xf).then_inc(xh_made, 1)
                dve.wait_ge(xh_made, j + 1)
                dve.tensor_tensor(xl[:, s], xf, xh[:, s], ALU.subtract).then_inc(x_ready, 1)

            def evacuate(j, s, turn):
                dve.wait_ge(y_ready, j + 1)
                if not isinstance(turn, int) or turn > 0:
                    dve.wait_ge(scattered[s], turn * 16)
                dve.tensor_copy(ys[:, s], ps[:, 7, 0:D]).then_inc(y_out, 1)

            def lower_hidden(j):
                for half in range(2):
                    part = slice(512 * half, 512 * half + 512)
                    dve.wait_ge(hh_made, j * 2 + (half + 1))
                    dve.scalar_tensor_tensor(out=hl[:, part], in0=ps[:, 2 + half], scalar=H_SCALE, in1=hh[:, part],
                                             op0=ALU.mult, op1=ALU.subtract).then_inc(split_done, 1)

            def step(j, s, turn):
                if not isinstance(j, int) or j > 1:
                    evacuate(j - 2, (s + 1) % 3, turn - (s < 2))
                if not isinstance(j, int) or j > 0:
                    lower_hidden(j - 1)
                prepare(j + 1, (s + 1) % 3)
                for n in late(j):
                    lower(n)

            prepare(0, 0)
            tiles_loop(dve, step)
            evacuate(TILES - 2, (TILES - 2) % 3, (TILES - 2) // 3)
            lower_hidden(TILES - 1)
            evacuate(TILES - 1, (TILES - 1) % 3, (TILES - 1) // 3)

            for g in range(NG):
                dve.wait_ge(y_in[g], 16 * TOP)
                for k in range(TOP):
                    for i in range(G):
                        row = xs[:, G * g + i]
                        ins = dve.scalar_tensor_tensor(out=row, in0=y_buf(g, k)[:, i], scalar=wts[:, k, G * g + i:G * g + i + 1],
                                                       in1=row, op0=ALU.mult, op1=ALU.add)
                    if k == 0:
                        ins.then_inc(half_done, 1)
                        dve.wait_ge(half_done, g + 1)
                ins.then_inc(out_made, 1)

        @block.tensor
        def _(pe):
            pe.wait_ge(ident_made, 1)
            pe.wait_ge(small_in, 16 * N_SMALL)
            for k in range(KD):
                pe.transpose(ps[:, 7, 12 * k:12 * k + 12], rows[0:12, k * P:(k + 1) * P], ident[0:12, 0:12])
            for k in range(KD):
                for b in range(B):
                    n = (k * B + b) * C
                    ins = pe.transpose(ps[:, 6, n:n + C], ctx_sb[0:C, b, k * P:(k + 1) * P], ident[0:C, 0:C])
            ins.then_inc(setup_pe, 1)
            for m in range(KD):
                for k in range(KD):
                    ins = pe.transpose(ps[:, 4, (m * KD + k) * P:(m * KD + k + 1) * P], wq_sb[:, k, m * P:(m + 1) * P], ident[:])
            ins.then_inc(setup_pe, 1)
            pe.wait_ge(setup_copied, 2)
            for m in range(KD):
                for k in range(KD):
                    ins = pe.matmul(ps[:, 5, m * B * C:(m + 1) * B * C], wk_sb[:, k, m * P:(m + 1) * P], ctxT[:, k],
                                    start=(k == 0), stop=(k == KD - 1))
            ins.then_inc(setup_pe, 1)

            def turn_x(g):
                pe.wait_ge(xn_made, g + 1)
                if g >= 2:
                    pe.wait_ge(uT_made, KD * (g - 1))
                for i in range(G):
                    for k in range(KD):
                        ins = pe.transpose(ps[:, k, i * P:(i + 1) * P], xn[:, i, k * P:(k + 1) * P], ident[:])
                ins.then_inc(x_turned, 1)

            def score(g):
                pe.wait_ge(xT_made, KD * (g + 1))
                if g >= 1:
                    pe.wait_ge(centred, g)
                for i in range(G):
                    o = ps[:, 2, i * C:(i + 1) * C]
                    b = g // 2
                    for k in range(KD):
                        pe.matmul(o, xT[:, k, i * P:(i + 1) * P], gk[:, k, b * C:(b + 1) * C], start=(k == 0), stop=False)
                    ins = pe.matmul(o, ones_f[0:1, :], s_bias[:, b * C:(b + 1) * C], start=False, stop=True)
                ins.then_inc(scored, 1)

            def attend(g):
                pe.wait_ge(exped, g + 1)
                for i in range(G):
                    ins = pe.transpose(ps[0:C, 3, i * P:(i + 1) * P], pr[:, g % 2, i], ident[:])
                ins.then_inc(p_turned, 1)
                pe.wait_ge(pT_made, g + 1)
                if g >= 1:
                    pe.wait_ge(x2_made, g)
                for i in range(G):
                    ins = pe.matmul(ps[:, 4 + i // 2, D * (i % 2):D * (i % 2) + D], pT[0:C, i * P:(i + 1) * P],
                                    v_sb[0:C, (g // 2) * D:(g // 2 + 1) * D], start=True, stop=True)
                ins.then_inc(attended, 1)

            def route(g):
                pe.wait_ge(u_made, g + 1)
                pe.wait_ge(xT_made, KD * min(g + 2, NG))
                for i in range(G):
                    for k in range(KD):
                        ins = pe.transpose(ps[:, k, i * P:(i + 1) * P], ub[:, g % 2, i, k * P:(k + 1) * P], ident[:])
                ins.then_inc(u_turned, 1)
                pe.wait_ge(uT_made, KD * (g + 1))
                if g >= 1:
                    pe.wait_ge(logits_read, g)
                for i in range(G):
                    o = ps[:, 6, i * E:(i + 1) * E]
                    for k in range(KD):
                        pe.matmul(o, uT[:, k, i * P:(i + 1) * P], rg[:, k], start=(k == 0), stop=False)
                    ins = pe.matmul(o, ones_f[0:1, :], r_bias[:], start=False, stop=True)
                ins.then_inc(logits_done, 1)

            turn_x(0)
            pe.wait_ge(setup_copied, 5)
            for k in range(KD):
                for m in range(KD):
                    ins = pe.matmul(ps[:, 4, k * B * C:(k + 1) * B * C], wqT[:, m, k * P:(k + 1) * P], kT[:, m],
                                    start=(m == 0), stop=(m == KD - 1))
            ins.then_inc(setup_pe, 1)
            pe.wait_ge(const_made, 3)
            for m in range(KD):
                pe.matmul(ps[0:1, 7, 32:32 + B * C], cols[:, m, 0:1], kT[:, m], start=(m == 0), stop=(m == KD - 1))
            for k in range(KD):
                pe.matmul(ps[0:1, 7, 200:208], cols[:, k, 3:4], cols[:, k, 4:12], start=(k == 0), stop=(k == KD - 1))
            for b in range(B):
                for k in range(KD):
                    pe.matmul(ps[0:C, 3, b * D:(b + 1) * D], ctxT[:, k, b * C:(b + 1) * C], wv_sb[:, k],
                              start=(k == 0), stop=False)
                pe.matmul(ps[0:C, 3, b * D:(b + 1) * D], ones_f[0:1, 0:C], bv_sb[:], start=False, stop=True)
            pe.wait_ge(gates_in, 32)
            pe.matmul(ps[:, 7, 210:212], ones_f[0:1, :], g_sb[:], start=True, stop=True).then_inc(setup_pe, 1)
            pe.wait_ge(setup_copied, 12)
            score(0)
            for t in range(1, NG + 2):
                if t <= NG:
                    attend(t - 1)
                if t >= 2:
                    route(t - 2)
                if t < NG:
                    turn_x(t)
                    score(t)

            pe.wait_ge(gates_made, 1)
            pe.wait_ge(ranked, NG)
            pe.matmul(ps[:, 7, 0:NT * E], before[:], sel_sum[:], start=True, stop=True)
            pe.matmul(ps[:, 7, NT * E:2 * NT * E], ones_b[:], sel_sum[:], start=True, stop=True).then_inc(counted, 1)
            for n in range(PAIRS):
                if n % 8 == 0:
                    pe.wait_ge(coded_made, n // 8 + 1)
                ins = pe.matmul(ps[:, 7, 256:256 + 2 * TILES], at_lane[:, n],
                                coded[:, n // NT, n % NT].rearrange("p c a -> p (c a)"),
                                start=(n == 0), stop=(n == PAIRS - 1))
            ins.then_inc(coded_out, 1)

            def turn_rows(j, s, turn):
                pe.wait_ge(gathered[s], (turn + 1) * 16)
                if not isinstance(j, int) or j > 0:
                    pe.wait_ge(x_ready, j)
                for k in range(KD):
                    ins = pe.transpose(ps[:, 6, k * P:(k + 1) * P], ug[:, s, k * P:(k + 1) * P], ident[:])
                ins.then_inc(uT_ready, 1)

            def hidden(j, s, at):
                pe.wait_ge(x_ready, j + 1)
                if j_of(j) is not None:
                    pe.wait_ge(w_lo_made, 2 * min(j_of(j), E - 1) + 2)
                for half in range(2):
                    o = ps[:, half]
                    for k in range(KD):
                        part = bass.ds(at + (k * H + half * 512), 512)
                        pe.matmul(o, xh[:, s, k], w_hi[:, part], start=(k == 0), stop=False)
                        pe.matmul(o, xh[:, s, k], w_lo[:, part], start=False, stop=False)
                        ins = pe.matmul(o, xl[:, s, k], w_hi[:, part], start=False, stop=(k == KD - 1))
                    ins.then_inc(h_ready, 1)

            def turn_hidden(j):
                for c in range(HC):
                    if c % 4 == 0:
                        pe.wait_ge(silu_done, j * 2 + (c // 4 + 1))
                    ins = pe.transpose(ps[:, 2 + c // 4, (c % 4) * P:(c % 4 + 1) * P], hs[:, c * P:(c + 1) * P], ident[:])
                    if c % 4 == 3:
                        ins.then_inc(hT_ready, 1)

            def back(j, at):
                pe.wait_ge(split_done, j * 2 + 2)
                if not isinstance(j, int) or j > 0:
                    pe.wait_ge(y_out, j)
                o = ps[:, 7, 0:D]
                for c in range(HC):
                    part = bass.ds(at + (CHUNK + c * D), D)
                    hi, lo = hh[:, c * P:(c + 1) * P], hl[:, c * P:(c + 1) * P]
                    pe.matmul(o, hi, w_hi[:, part], start=(c == 0), stop=False)
                    pe.matmul(o, hi, w_lo[:, part], start=False, stop=False)
                    ins = pe.matmul(o, lo, w_hi[:, part], start=False, stop=(c == HC - 1))
                ins.then_inc(y_ready, 1)

            def j_of(j):
                return j if isinstance(j, int) else None

            def place(j):
                return nc.values_load(etab[0:1, bass.ds(j, 1)] if not isinstance(j, int) else etab[0:1, j:j + 1],
                                      engines=(mybir.EngineType.PE,), min_val=0, max_val=(E - 1) * 2 * CHUNK,
                                      skip_runtime_bounds_check_because="the table's entries are clamped to the experts")

            known = {}

            def step(j, s, turn):
                turn_rows(j + 1, (s + 1) % 3, turn + (s == 2))
                if j_of(j) != 0:
                    turn_hidden(j - 1)
                if j_of(j) is None and s == 0:
                    pe.wait_ge(w_lo_made, NW)
                    known["last"] = place(j - 1)
                at = place(j)
                hidden(j, s, at)
                if j_of(j) != 0:
                    back(j - 1, known["last"])
                known["last"] = at

            pe.wait_ge(index_made, 1)
            turn_rows(0, 0, 0)
            tiles_loop(pe, step)
            turn_hidden(TILES - 1)
            back(TILES - 1, place(TILES - 1))


_INS = ["x", "ctx_1024", "g_xattn", "g_ffn", "L0_xattn_Wq", "L0_xattn_bq", "L0_xattn_Wk", "L0_xattn_bk",
        "L0_xattn_Wv", "L0_xattn_bv", "L0_ffn_gamma", "L0_ffn_beta", "L0_ffn_router_w", "L0_ffn_W1", "L0_ffn_W2"]


def kernel(**inputs):
    import numpy as _np
    import concourse.bacc as _bacc
    from concourse import mybir as _mybir
    from concourse.bass_utils import run_bass_kernel_spmd as _run

    nc = _bacc.Bacc("TRN2", target_bir_lowering=False, num_devices=1)
    arrays, args = {}, []
    for name in _INS:
        a = _np.ascontiguousarray(inputs[name])
        arrays[f"in_{name}"] = a
        args.append(nc.dram_tensor(f"in_{name}", a.shape, _mybir.dt.from_np(a.dtype), kind="ExternalInput").ap())
    out = nc.dram_tensor("out_0", (B, S, D), F32, kind="ExternalOutput").ap()
    gated_attention_moe(nc, *args, out)
    r = _run(nc, [arrays], core_ids=[0])
    return r.results[0]["out_0"]
```

```python
from contextlib import ExitStack

import concourse.bass as bass
from concourse import mybir

ALU = mybir.AluOpType
ACT = mybir.ActivationFunctionType
AX = mybir.AxisListType
F32, F16, BF16, I32 = mybir.dt.float32, mybir.dt.float16, mybir.dt.bfloat16, mybir.dt.int32

P = 128
B, S, D = 2, 1024, 256
C = 77
KD = D // P
NT = B * S // P
G = 4
NG = NT // G
E, H = 8, 1024
HC = H // P
TOP = 2
PAIRS = TOP * NT
TILES = (TOP * B * S + E * (P - 1)) // P
EPS = 1e-5
TEMP = 1.5
BETA = 1.0 / D ** 0.5
FILL = [[1], [2], [3], [4, 5], [6, 7]]
LATE_UPPER = [[8, 9, 10], [], [11], [12], [13], [14], [15]]
LATE_LOWER = [[8, 9], [10], [11], [12], [13], [14], [15]]
W_SCALE, X_SCALE, H_SCALE = 64.0, 16.0, 16.0
CHUNK = KD * H
NW = 2 * E
NSTAGE = 3
PEELED = len(LATE_LOWER)
WARM = [20, [0, 10, 0, 0], 10, 14, 0, 4, 4]
UNUSED = TOP * B * S


SURE = 37


def gated_attention_moe(nc, x, ctx, g_x, g_f, wq, bq, wk, bk, wv, bv, gamma, beta, router, w1, w2, out):
    with ExitStack() as stack:
        def sb(name, shape, dt=F32):
            return stack.enter_context(nc.sbuf_tensor(name, shape, dt))

        def sem(name):
            return stack.enter_context(nc.semaphore(name))

        u_rows = nc.dram_tensor("u_rows", [B * S, D], F32, kind="Internal").ap()
        z_rows = nc.dram_tensor("z_rows", [B * S + P, D], F32, kind="Internal").ap()
        w_rows = nc.dram_tensor("w_rows", [UNUSED + P, 1], F32, kind="Internal").ap()

        ps = stack.enter_context(nc.psum_tensor("ps", [P, 8, 512], F32))

        w_hi = sb("w_hi", [P, NW * CHUNK], F16)
        w_lo = sb("w_lo", [P, NW * CHUNK], F16)
        stage = sb("stage", [P, NSTAGE, CHUNK])
        xs = sb("xs", [P, NT, D])
        arena = sb("arena", [P, 7168])

        def view(start, cols, dt=F32):
            return arena[:, start:start + cols].bitcast(dt) if dt != F32 else arena[:, start:start + cols]

        xT = view(1024, KD * 512).rearrange("p (k t) -> p k t", k=KD)
        uT = view(2048, KD * 512).rearrange("p (k t) -> p k t", k=KD)
        ub = view(3072, 2 * G * D).rearrange("p (n i d) -> p n i d", n=2, i=G)
        pr = view(5120, 2 * G * C).rearrange("p (n i c) -> p n i c", n=2, i=G)
        pT = view(5760, 512)
        late_hi = w_hi[:, (NW - 2) * CHUNK:].bitcast(F32)
        late_lo = w_lo[:, (NW - 2) * CHUNK:].bitcast(F32)
        wq_sb = late_lo[:, 0:512].rearrange("p (k n) -> p k n", k=KD)
        wk_sb = late_lo[:, 512:1024].rearrange("p (k n) -> p k n", k=KD)
        wv_sb = late_lo[:, 1024:1536].rearrange("p (k n) -> p k n", k=KD)
        wqT = late_lo[:, 1536:2048].rearrange("p (m d) -> p m d", m=KD)
        ctx_sb = late_hi[:, 0:512].rearrange("p (b d) -> p b d", b=B)
        xn = [ap.rearrange("p (i d) -> p i d", i=G) for ap in (view(0, G * D), late_lo[:, 0:G * D])]
        rows = late_hi[:, 512:768]
        ctxT = late_hi[:, 768:768 + KD * B * C].rearrange("p (k c) -> p k c", k=KD)
        kT = late_hi[:, 1088:1088 + KD * B * C].rearrange("p (k c) -> p k c", k=KD)
        at_tile = view(0, PAIRS * TILES // 2, BF16).rearrange("p (k t a) -> p k t a", k=TOP, t=NT)
        coded = view(640, PAIRS * 2 * TILES // 2, BF16).rearrange("p (k t c a) -> p k t c a", k=TOP, t=NT, c=2)
        at_lane = view(1920, PAIRS * P // 2, BF16).rearrange("p (n b) -> p n b", n=PAIRS)
        tot = view(3968, E * NT).rearrange("p (e t) -> p e t", e=E)
        cum = view(4096, E * NT).rearrange("p (e t) -> p e t", e=E)
        pos = view(4224, NT * E).rearrange("p (t e) -> p t e", e=E)
        picked = view(4352, PAIRS * E).rearrange("p (k t e) -> p k t e", k=TOP, t=NT)
        ecmp = view(4608, TILES * E)[0:1].rearrange("p (a e) -> p a e", a=TILES)
        slot = view(4920, 3 * PAIRS).rearrange("p (n c) -> p n c", n=3)
        slot_i = view(5016, 3 * PAIRS, I32).rearrange("p (n c) -> p n c", n=3)
        code = view(5112, 2 * TILES).rearrange("p (n c) -> p n c", n=2)
        dstf = view(5190, 2 * TILES).rearrange("p (n c) -> p n c", n=2)
        slot_i2 = view(5308, TILES, I32)
        etab_f = view(5268, TILES)[0:1]
        ug = view(0, 3 * D).rearrange("p (s d) -> p s d", s=3)
        xf = view(768, D).rearrange("p (k t) -> p k t", k=KD)
        xh = view(1024, 3 * D // 2, F16).rearrange("p (s k t) -> p s k t", s=3, k=KD)
        xl = view(1408, 3 * D // 2, F16).rearrange("p (s k t) -> p s k t", s=3, k=KD)
        hs = view(1792, H)
        hh = view(2816, H // 2, F16)
        hl = view(3328, H // 2, F16)
        ys = view(3840, 3 * D).rearrange("p (s d) -> p s d", s=3)

        ident = sb("ident", [P, P])
        before = sb("before", [P, P], BF16)
        ones_b = sb("ones_b", [P, P], BF16)
        ones_f = sb("ones_f", [P, P])
        lane_no = sb("lane_no", [P, P], BF16)
        tile_no = sb("tile_no", [P, TILES])
        choice_lane = sb("choice_lane", [P, TOP])
        expert_no = sb("expert_no", [P, G, E])
        ttile_no = sb("ttile_no", [P, NT])
        unused_row = sb("unused_row", [P, TILES])
        expo = sb("expo", [P, G])
        vectors = sb("vectors", [P, D + 2 + B * C + E])
        bv_sb, g_sb = vectors[:, 0:D], vectors[:, D:D + 2]
        s_bias = vectors[:, D + 2:D + 2 + B * C]
        r_bias = vectors[:, D + 2 + B * C:]
        tg = sb("tg", [P, 2])
        cols = sb("cols", [P, KD, 12])
        v_sb = sb("v_sb", [P, B * D])
        gk = sb("gk", [P, KD, B * C])
        rg = sb("rg", [P, KD, E])
        gb16 = sb("gb16", [P, KD, 2])
        stats = sb("stats", [P, G, 6])
        mv = sb("mv", [P, 2, 2, G, 2])
        var1 = sb("var1", [P, 2, G])
        rstd1 = sb("rstd1", [P, 2, G])
        var2 = sb("var2", [P, 2, NG, G])
        rstd2 = sb("rstd2", [P, 2, NG, G])
        less_mean = sb("less_mean", [P, NG, G])
        u_bias = sb("u_bias", [P, NG, G])
        res_scale = sb("res_scale", [P, 3, NG, G])
        x_bias = res_scale[:, 0, 0:2]
        small = sb("small", [P, 4, G])
        lg = sb("lg", [P, G, E])
        top = sb("top", [P, NT, E])
        top_no = sb("top_no", [P, NT, E], mybir.dt.uint32)
        sel = sb("sel", [P, TOP, NT, E])
        sel_sum = sb("sel_sum", [P, NT * E], BF16)
        edge = sb("edge", [P, E + 1])
        ecnt = sb("ecnt", [P, 4, E])
        ecnt_i = sb("ecnt_i", [P, 2, E], I32)
        pair = sb("pair", [P, TILES], I32)
        src = sb("src", [P, TILES], I32)
        dst = sb("dst", [P, TILES], I32)
        slot_w = sb("slot_w", [P, 3])
        etab = sb("etab", [1, TILES + 1], I32)
        smx = sb("smx", [P, 2, NT])
        wts = sb("wts", [P, TOP, NT])

        x_in = [sem(f"x_in{g}") for g in range(NG)]
        rows_in, wq_in, wk_in, wv_in, vectors_in = (sem(n) for n in ("rows_in", "wq_in", "wk_in", "wv_in", "vectors_in"))
        x_biased = sem("x_biased")
        w_in = [sem(f"w_in{n}") for n in range(NSTAGE)]
        const_made, const_chain = sem("const_made"), sem("const_chain")
        w_hi_made, w_lo_made = sem("w_hi_made"), sem("w_lo_made")
        setup_pe, setup_copied, vectors_made = sem("setup_pe"), sem("setup_copied"), sem("vectors_made")
        ident_made, gates_made = sem("ident_made"), sem("gates_made")
        stats1, pow1, xn_made = sem("stats1"), sem("pow1"), sem("xn_made")
        x_turned, xT_made = sem("x_turned"), sem("xT_made")
        scored, centred, exped = sem("scored"), sem("centred"), sem("exped")
        p_turned, pT_made, attended = sem("p_turned"), sem("pT_made"), sem("attended")
        x2_made, stats2, pow_chain, pow2, pow3, u_made = (sem(n) for n in ("x2_made", "stats2", "pow_chain", "pow2", "pow3", "u_made"))
        warm_made, res_coded = sem("warm_made"), sem("res_coded")
        u_written = [sem(f"u_written{g}") for g in range(NG)]
        u_turned, uT_made = sem("u_turned"), sem("uT_made")
        logits_done, logits_read, ranked = sem("logits_done"), sem("logits_read"), sem("ranked")
        counted, coded_made, coded_out, index_made = (sem(n) for n in ("counted", "coded_made", "coded_out", "index_made"))
        res_made = sem("res_made")
        w_centred, w_exped = sem("w_centred"), sem("w_exped")
        at_tile_made, lanes_made, etab_made, codes_made = (
            sem(n) for n in ("at_tile_made", "lanes_made", "etab_made", "codes_made"))
        dve_step = sem("dve_step")
        gathered = [sem(f"gathered{s}") for s in range(3)]
        scattered = [sem(f"scattered{s}") for s in range(3)]
        uT_ready, xf_made, xh_made, x_ready = sem("uT_ready"), sem("xf_made"), sem("xh_made"), sem("x_ready")
        h_ready, silu_done, hT_ready = sem("h_ready"), sem("silu_done"), sem("hT_ready")
        hh_made, split_done = sem("hh_made"), sem("split_done")
        y_ready, y_out = sem("y_ready"), sem("y_out")
        z_written, weights_made, w_written, dst_made, all_added, out_written = (
            sem(n) for n in ("z_written", "weights_made", "w_written", "dst_made", "all_added", "out_written"))
        weighed = [sem(f"weighed{s}") for s in range(3)]

        N_ROWS, N_VECTORS = 6, 3
        N_CONST = 10

        x_view = x.rearrange("b (p i) d -> b p i d", p=P)
        u_view = u_rows.rearrange("(p t) d -> p t d", p=P)

        def group(ap, g):
            return ap[g // 2, :, G * (g % 2):G * (g % 2) + G, :]

        def weight_source(n):
            e = n // 2
            if n % 2 == 0:
                return w1[e].rearrange("(k p) n -> p k n", p=P)
            return w2[e].rearrange("(c p) n -> p c n", p=P)

        def run_tiles(eng, engine, step, finish):
            for j in range(PEELED):
                step(j, j % 3, j // 3)
            turns = (SURE - PEELED) // 3
            with eng.Fori(0, turns) as i:
                for t in range(3):
                    step(i * 3 + (PEELED + t), (PEELED + t) % 3, i + (PEELED + t) // 3)
            for j in range(PEELED + 3 * turns, SURE):
                step(j, j % 3, j // 3)
            eng.wait_ge(etab_made, 1)
            with eng.If(tiles_used(engine) > SURE):
                for j in range(SURE, TILES):
                    step(j, j % 3, j // 3)
                finish(TILES)
            with eng.Else():
                finish(SURE)

        def tiles_used(engine):
            return nc.values_load(etab[0:1, TILES:TILES + 1], engines=(engine,), min_val=0, max_val=TILES,
                                  skip_runtime_bounds_check_because="a count of tiles, which the shapes bound")

        def late(which, j):
            return which[j] if isinstance(j, int) and j < PEELED else []

        block = stack.enter_context(nc.Block())

        @block.sync
        def _(sp):
            def load_x(g):
                sp.dma_start(xs[:, G * g:G * g + G, :], group(x_view, g)).then_inc(x_in[g], 16)

            load_x(0)
            for w_sb, w, landed in ((wk_sb, wk, wk_in), (wq_sb, wq, wq_in), (wv_sb, wv, wv_in)):
                sp.dma_start(w_sb, w.rearrange("(k p) n -> p k n", p=P)).then_inc(landed, 16)
            load_x(1)
            for g in range(2, NG):
                load_x(g)
            for n in range(NW):
                if n >= NSTAGE:
                    if n > NSTAGE:
                        sp.wait_ge(w_hi_made, n - NSTAGE)
                    sp.wait_ge(w_lo_made, n - NSTAGE + 1)
                shape = "p (k n) -> p k n"
                sp.dma_start(stage[:, n % NSTAGE].rearrange(shape, k=KD if n % 2 == 0 else HC),
                             weight_source(n)).then_inc(w_in[n % NSTAGE], 16)
            sp.wait_ge(all_added, 1)
            for b in range(B):
                sp.dma_start(out[b].rearrange("(p i) d -> p i d", p=P),
                             z_rows[0:B * S].rearrange("(p b i) d -> b p i d", p=P, b=B)[b]).then_inc(out_written, 16)
            sp.wait_ge(out_written, 16 * B)

        @block.gpsimd
        def _(pool):
            pool.memset(ident[:], 0.0).then_inc(const_chain, 1)
            pool.wait_ge(const_chain, 1)
            pool.affine_select(out=ident[:], in_=ident[:], compare_op=ALU.not_equal, fill=1.0, base=0,
                               pattern=[[-1, P]], channel_multiplier=1).then_inc(ident_made, 1)
            pool.memset(vectors[:], 0.0).then_inc(vectors_made, 1)
            pool.memset(ones_b[:], 1.0).then_inc(warm_made, 1)
            pool.wait_ge(vectors_made, 1)
            pool.dma_start(bv_sb[0:1], bv.unsqueeze(0)).then_inc(vectors_in, 16)
            pool.dma_start(g_sb[0:1, 0:1], g_x.unsqueeze(0)).then_inc(vectors_in, 16)
            pool.dma_start(g_sb[0:1, 1:2], g_f.unsqueeze(0)).then_inc(vectors_in, 16)
            pool.memset(expo[:], -0.5).then_inc(const_made, 1)
            pool.memset(ones_f[:], 1.0).then_inc(const_made, 1)
            pool.wait_ge(const_made, 1)

            def power_x(g):
                pool.wait_ge(stats1, g + 1)
                pool.tensor_tensor(rstd1[:, g % 2], var1[:, g % 2], expo[:], ALU.pow).then_inc(pow1, 1)
                if g >= 2:
                    pool.wait_ge(pow1, g + 1)
                    pool.tensor_tensor(x_bias[:, g % 2], x_bias[:, g % 2], rstd1[:, g % 2], ALU.mult).then_inc(x_biased, 1)

            def power_x2(g):
                pool.wait_ge(stats2, g + 1)
                pool.tensor_tensor(rstd2[:, 0, g], var2[:, 0, g], expo[:], ALU.pow).then_inc(pow_chain, 1)
                pool.wait_ge(pow_chain, g + 1)
                pool.tensor_tensor(u_bias[:, g], less_mean[:, g], rstd2[:, 0, g], ALU.mult).then_inc(pow2, 1)
                pool.tensor_tensor(rstd2[:, 1, g], var2[:, 1, g], expo[:], ALU.pow).then_inc(pow3, 1)

            power_x(0)
            power_x(1)
            pool.memset(edge[:, 0:1], 0.0).then_inc(const_made, 1)
            pool.memset(before[:], 1.0).then_inc(const_chain, 1)
            pool.wait_ge(const_chain, 2)
            pool.affine_select(out=before[:], in_=before[:], compare_op=ALU.is_gt, fill=0.0, base=0,
                               pattern=[[1, P]], channel_multiplier=-1).then_inc(const_made, 1)

            def numbers(ap, pattern, base, channel):
                pool.iota(ap, pattern=pattern, base=base, channel_multiplier=channel,
                          allow_small_or_imprecise_dtypes=True).then_inc(const_made, 1)

            numbers(lane_no[:], [[1, P]], 0, 0)
            numbers(tile_no[:], [[1, TILES]], 0, 0)
            numbers(choice_lane[:], [[P, TOP]], 1, 1)
            numbers(ttile_no[:], [[1, NT]], 0, 0)
            numbers(expert_no[:], [[0, G], [1, E]], 0, 0)
            numbers(unused_row[:], [[0, TILES]], UNUSED + NT, 1)
            for t in range(NG):
                if t + 2 < NG:
                    power_x(t + 2)
                power_x2(t)

            for k in range(TOP):
                pool.wait_ge(at_tile_made, k + 1)
                pool.tensor_tensor(coded[:, k, :, 1], at_tile[:, k],
                                   ttile_no[:].unsqueeze(2).to_broadcast([P, NT, TILES]), ALU.mult).then_inc(codes_made, 1)

            def gather(j):
                col = min(j, TILES - 1)
                pool.indirect_dma_start(out=ug[:, j % 3], out_offset=None, in_=u_rows,
                                        in_offset=bass.IndirectOffsetOnAxis(ap=src[:, col:col + 1], axis=0)
                                        ).then_inc(gathered[j % 3], 16)

            for g in range(NG):
                pool.wait_ge(u_written[g], 16)
            pool.wait_ge(index_made, 1)
            for j in range(3):
                gather(j)

            def weigh(j):
                pool.indirect_dma_start(out=slot_w[:, j % 3:j % 3 + 1], out_offset=None, in_=w_rows,
                                        in_offset=bass.IndirectOffsetOnAxis(ap=pair[:, j:j + 1], axis=0)
                                        ).then_inc(weighed[j % 3], 16)

            pool.wait_ge(w_written, 32)
            for j in range(3):
                weigh(j)
            pool.wait_ge(z_written, 32)
            pool.wait_ge(dst_made, 1)

            def add_rows(j):
                pool.wait_ge(y_out, j + 1)
                if j > 0:
                    pool.wait_ge(scattered[(j - 1) % 3], 16 * ((j - 1) // 3 + 1))
                pool.indirect_dma_start(out=z_rows, out_offset=bass.IndirectOffsetOnAxis(ap=dst[:, j:j + 1], axis=0),
                                        in_=ys[:, j % 3], in_offset=None, compute_op=ALU.add).then_inc(scattered[j % 3], 16)

            for j in range(SURE):
                if j + 3 < TILES:
                    pool.wait_ge(uT_ready, j + 1)
                    gather(j + 3)
                add_rows(j)
                if j + 3 < TILES:
                    weigh(j + 3)
            pool.wait_ge(etab_made, 1)
            with pool.If(tiles_used(mybir.EngineType.Pool) > SURE):
                pool.wait_ge(uT_ready, TILES - 2)
                gather(TILES)
                for j in range(SURE, TILES):
                    add_rows(j)
                pool.wait_ge(scattered[(TILES - 1) % 3], 16 * ((TILES - 1) // 3 + 1))
            with pool.Else():
                pool.wait_ge(scattered[(SURE - 1) % 3], 16 * ((SURE - 1) // 3 + 1))
                for j in range(SURE, TILES):
                    pool.wait_ge(gathered[j % 3], 16 * (j // 3 + 1))
                    pool.wait_ge(weighed[j % 3], 16 * (j // 3 + 1))
            pool.memset(edge[:, E:E + 1], 0.0).then_inc(all_added, 1)

        @block.scalar
        def _(act):
            def upper(n):
                act.wait_ge(w_in[n % NSTAGE], 16 * (n // NSTAGE + 1))
                act.activation(w_hi[:, n * CHUNK:(n + 1) * CHUNK], stage[:, n % NSTAGE], ACT.Copy,
                               scale=W_SCALE).then_inc(w_hi_made, 1)

            def copy(to, of):
                act.activation(to, of, ACT.Copy).then_inc(setup_copied, 1)

            def turned_x(g):
                act.wait_ge(x_turned, g + 1)
                for k in range(KD):
                    act.activation(xT[:, k], ps[:, k], ACT.Copy).then_inc(xT_made, 1)

            def load_rows(to, of):
                act.dma_start(to, of).then_inc(rows_in, 16)

            load_rows(ctx_sb[0:C], ctx.rearrange("b c d -> c b d"))
            load_rows(rows[0:1], bq.unsqueeze(0))
            load_rows(rows[1:2], bk.unsqueeze(0))
            load_rows(rows[2:3], gamma.unsqueeze(0))
            load_rows(rows[3:4], beta.unsqueeze(0))
            load_rows(rows[4:12], router)

            act.wait_ge(setup_pe, 1)
            copy(cols[:].rearrange("p k n -> p (k n)"), ps[:, 7, 0:24])
            copy(ctxT, ps[:, 6, 0:KD * B * C].rearrange("p (k c) -> p k c", k=KD))
            act.wait_ge(setup_pe, 2)
            copy(wqT, ps[:, 4].rearrange("p (m d) -> p m d", m=KD))
            act.wait_ge(setup_pe, 3)
            act.wait_ge(setup_copied, 1)
            for m in range(KD):
                act.activation(kT[:, m], ps[:, 5, m * B * C:(m + 1) * B * C], ACT.Identity,
                               bias=cols[:, m, 1:2]).then_inc(setup_copied, 1)
            turned_x(0)
            act.wait_ge(setup_pe, 4)
            copy(gk[:], ps[:, 4, 0:KD * B * C].rearrange("p (k c) -> p k c", k=KD))
            act.wait_ge(vectors_made, 1)
            copy(s_bias[0:1], ps[0:1, 7, 32:32 + B * C])
            copy(r_bias[0:1], ps[0:1, 7, 200:208])
            for k in range(KD):
                act.activation(rg[:, k], cols[:, k, 4:12], ACT.Copy, scale=cols[:, k, 2:3]).then_inc(setup_copied, 1)
            act.activation(gb16[:], cols[:, :, 2:4], ACT.Copy, scale=X_SCALE).then_inc(setup_copied, 1)

            def norm_x(g):
                act.wait_ge(x_biased, g - 1)
                act.wait_ge(x_turned, g - 1)
                for i in range(G):
                    ins = act.activation(xn[g % 2][:, i], xs[:, G * g + i], ACT.Identity, bias=x_bias[:, g % 2, i:i + 1],
                                         scale=rstd1[:, g % 2, i:i + 1])
                ins.then_inc(xn_made, 1)

            def norm_u(g):
                act.wait_ge(pow2, g + 1)
                if g >= 2:
                    act.wait_ge(u_written[g - 2], 16)
                for i in range(G):
                    ins = act.activation(ub[:, g % 2, i], xs[:, G * g + i], ACT.Identity, bias=u_bias[:, g, i:i + 1],
                                         scale=rstd2[:, 0, g, i:i + 1])
                ins.then_inc(u_made, 1)

            def turned_u(g):
                act.wait_ge(u_made, g + 1)
                act.dma_start(u_view[:, G * g:G * g + G, :], ub[:, g % 2]).then_inc(u_written[g], 16)
                act.wait_ge(u_turned, g + 1)
                for k in range(KD):
                    act.activation(uT[:, k], ps[:, 6 + k], ACT.Copy).then_inc(uT_made, 1)

            for n in FILL[0]:
                upper(n)
            for t in range(NG):
                act.wait_ge(centred, t + 1)
                act.activation(pr[:, t % 2], pr[:, t % 2], ACT.Exp, scale=BETA).then_inc(exped, 1)
                if t == 0:
                    act.wait_ge(setup_pe, 5)
                    copy(v_sb[0:C], ps[0:C, 3])
                    act.activation(tg[:], ps[:, 5, 400:402], ACT.Tanh).then_inc(gates_made, 1)
                act.wait_ge(p_turned, t + 1)
                act.activation(pT[0:C], ps[0:C, 3], ACT.Copy).then_inc(pT_made, 1)
                if t + 1 < NG:
                    turned_x(t + 1)
                if t >= 1:
                    norm_u(t - 1)
                    if t == 1:
                        norm_x(3)
                    else:
                        upper(FILL[t + 1][0])
                    turned_u(t - 1)
                for n in FILL[t + 1][t >= 2:]:
                    upper(n)
                if t == 0:
                    norm_x(2)
            norm_u(NG - 1)
            turned_u(NG - 1)

            act.wait_ge(res_coded, 1)
            for t in range(NT):
                act.activation(xs[:, t], xs[:, t], ACT.Identity, bias=res_scale[:, 2, t // G, t % G:t % G + 1],
                               scale=res_scale[:, 1, t // G, t % G:t % G + 1]).then_inc(res_made, 1)
            act.wait_ge(res_made, NT)
            act.dma_start(z_rows[0:B * S].rearrange("(p t) d -> p t d", p=P), xs[:]).then_inc(z_written, 16)
            act.dma_start(z_rows[B * S:B * S + P], xs[:, 0]).then_inc(z_written, 16)
            for k in range(TOP):
                act.wait_ge(at_tile_made, k + 1)
                act.activation(coded[:, k, :, 0], at_tile[:, k], ACT.Copy, scale=choice_lane[:, k:k + 1]).then_inc(lanes_made, 1)
            act.wait_ge(w_centred, 1)
            act.activation(top[:], top[:], ACT.Exp, scale=1.0 / TEMP).then_inc(w_exped, 1)

            def upper_hidden(j):
                for half in range(2):
                    part = slice(512 * half, 512 * half + 512)
                    act.wait_ge(hT_ready, j * 2 + (half + 1))
                    act.activation(hh[:, part], ps[:, 2 + half], ACT.Copy, scale=H_SCALE).then_inc(hh_made, 1)

            def step(j, s, turn):
                if not isinstance(j, int) or j > 0:
                    upper_hidden(j - 1)
                for half in range(2):
                    act.wait_ge(h_ready, j * 2 + (half + 1))
                    act.activation(hs[:, 512 * half:512 * half + 512], ps[:, half], ACT.Silu,
                                   scale=1.0 / (W_SCALE * X_SCALE)).then_inc(silu_done, 1)
                for n in late(LATE_UPPER, j + 1):
                    upper(n)

            act.activation(small[:, 0, 0:1], edge[:, 0:1], ACT.Silu)
            act.wait_ge(weights_made, 1)
            act.dma_start(w_rows[0:UNUSED].rearrange("(k p t) o -> p k (t o)", k=TOP, p=P), wts[:]).then_inc(w_written, 16)
            act.dma_start(w_rows[UNUSED:UNUSED + P], edge[:, 0:1]).then_inc(w_written, 16)
            for n in late(LATE_UPPER, 0):
                upper(n)

            def finish(n):
                upper_hidden(n - 1)

            run_tiles(act, mybir.EngineType.Activation, step, finish)

        @block.vector
        def _(dve):
            steps = [0]

            def link(ins):
                steps[0] += 1
                ins.then_inc(dve_step, 1)
                dve.wait_ge(dve_step, steps[0])

            def lower(n):
                if n > 0:
                    dve.wait_ge(w_hi_made, n)
                dve.scalar_tensor_tensor(out=w_lo[:, n * CHUNK:(n + 1) * CHUNK], in0=stage[:, n % NSTAGE],
                                         scalar=W_SCALE, in1=w_hi[:, n * CHUNK:(n + 1) * CHUNK],
                                         op0=ALU.mult, op1=ALU.subtract).then_inc(w_lo_made, 1)

            def moments(g, which):
                for i in range(G):
                    ins = dve.bn_stats(stats[:, i], xs[:, G * g + i])
                link(ins)
                for i in range(G):
                    ins = dve.bn_aggr(mv[:, which, g % 2, i], stats[:, i])
                link(ins)

            def variance_x(g):
                dve.wait_ge(x_in[g], 16)
                moments(g, 0)
                dve.tensor_scalar(x_bias[:, g % 2], mv[:, 0, g % 2, :, 0], -1.0, None, ALU.mult)
                dve.tensor_scalar(var1[:, g % 2], mv[:, 0, g % 2, :, 1], EPS, None, ALU.add).then_inc(stats1, 1)

            def norm_x(g):
                if g == 1:
                    dve.wait_ge(setup_pe, 3)
                dve.wait_ge(pow1, g + 1)
                for i in range(G):
                    ins = dve.tensor_scalar(xn[g % 2][:, i], xs[:, G * g + i], mv[:, 0, g % 2, i, 0:1],
                                            rstd1[:, g % 2, i:i + 1], ALU.subtract, ALU.mult)
                ins.then_inc(xn_made, 1)

            def centre(g):
                dve.wait_ge(scored, g + 1)
                scores = ps[:, 2, 0:G * C].rearrange("p (i c) -> p i c", i=G)
                link(dve.tensor_reduce(small[:, 0], scores, AX.X, ALU.max))
                dve.tensor_tensor(pr[:, g % 2], scores, small[:, 0].unsqueeze(2).to_broadcast([P, G, C]),
                                  ALU.subtract).then_inc(centred, 1)

            def attend(g):
                dve.wait_ge(exped, g + 1)
                link(dve.tensor_reduce(small[:, 1], pr[:, g % 2], AX.X, ALU.add))
                link(dve.reciprocal(small[:, 2], small[:, 1]))
                if g == 0:
                    dve.wait_ge(gates_made, 1)
                link(dve.tensor_scalar(small[:, 3], small[:, 2], tg[:, 0:1], None, ALU.mult))
                dve.wait_ge(attended, g + 1)
                for i in range(G):
                    row = xs[:, G * g + i]
                    ins = dve.scalar_tensor_tensor(out=row, in0=ps[:, 4 + i // 2, D * (i % 2):D * (i % 2) + D],
                                                   scalar=small[:, 3, i:i + 1], in1=row, op0=ALU.mult, op1=ALU.add)
                ins.then_inc(x2_made, 1)
                dve.wait_ge(x2_made, g + 1)
                moments(g, 1)
                mean, var = mv[:, 1, g % 2, :, 0], mv[:, 1, g % 2, :, 1]
                dve.tensor_scalar(var2[:, 0, g], var, 1.0 + EPS, EPS * EPS, ALU.mult, ALU.add)
                dve.tensor_scalar(less_mean[:, g], mean, -1.0, None, ALU.mult)
                dve.tensor_scalar(var2[:, 1, g], var, EPS, None, ALU.add).then_inc(stats2, 1)

            def read_logits(g):
                dve.wait_ge(logits_done, g + 1)
                dve.tensor_copy(lg[:], ps[:, 7, 0:G * E].rearrange("p (i e) -> p i e", i=G)).then_inc(logits_read, 1)

            def choose(g):
                own = slice(G * g, G * g + G)
                dve.wait_ge(logits_read, g + 1)
                for i in range(G):
                    ins = dve.max(top[:, G * g + i], lg[:, i])
                link(ins)
                for i in range(G):
                    ins = dve.max_index(top_no[:, G * g + i], top[:, G * g + i], lg[:, i])
                link(ins)
                for k in range(TOP):
                    ins = dve.tensor_tensor(sel[:, k, own], expert_no[:],
                                            top_no[:, own, k:k + 1].to_broadcast([P, G, E]), ALU.is_equal)
                link(ins)
                dve.tensor_tensor(sel_sum[:, G * E * g:G * E * (g + 1)].rearrange("p (i e) -> p i e", i=G),
                                  sel[:, 0, own], sel[:, 1, own], ALU.add).then_inc(ranked, 1)

            variance_x(0)
            variance_x(1)
            norm_x(0)
            norm_x(1)
            dve.wait_ge(w_in[0], 16)
            link(dve.tensor_scalar(w_hi[:, 0:CHUNK], stage[:, 0], W_SCALE, None, ALU.mult))
            lower(0)
            for t in range(NG):
                centre(t)
                if t + 2 < NG:
                    variance_x(t + 2)
                for n in FILL[t]:
                    lower(n)
                if t == 2:
                    dve.wait_ge(const_made, N_CONST)
                if t >= 2:
                    read_logits(t - 2)
                if t == 2:
                    choose(0)
                attend(t)
            choose(NG - 3)
            read_logits(NG - 2)
            choose(NG - 2)
            dve.wait_ge(pow3, NG)
            link(dve.tensor_scalar(res_scale[:, 0], rstd2[:, 1], tg[:, 1:2], None, ALU.mult))
            dve.tensor_scalar(res_scale[:, 1], res_scale[:, 0], 1.0, None, ALU.add)
            dve.tensor_tensor(res_scale[:, 2], res_scale[:, 0], less_mean[:], ALU.mult).then_inc(res_coded, 1)
            for n in FILL[NG]:
                lower(n)
            read_logits(NG - 1)
            choose(NG - 1)

            for g in (NG - 2, NG - 1):
                dve.wait_ge(u_written[g], 16)
            dve.wait_ge(counted, 1)
            link(dve.tensor_copy(tot, ps[:, 7, NT * E:2 * NT * E].rearrange("p (t e) -> p e t", e=E)))
            flat = "p e t -> p (e t)"
            link(dve.tensor_tensor_scan(cum.rearrange(flat), ones_f[:], tot.rearrange(flat), 0.0, ALU.mult, ALU.add))
            link(dve.tensor_copy(edge[:, 1:E + 1], cum[:, :, NT - 1]))
            link(dve.tensor_tensor(ecnt[:, 0], edge[:, 1:E + 1], edge[:, 0:E], ALU.subtract))
            link(dve.tensor_scalar(ecnt_i[:, 0], ecnt[:, 0], float(P - 1), None, ALU.add))
            link(dve.tensor_scalar(ecnt_i[:, 1], ecnt_i[:, 0], 7, None, ALU.arith_shift_right))
            link(dve.tensor_scalar(ecnt[:, 1], ecnt_i[:, 1], 1.0, None, ALU.max))
            link(dve.tensor_tensor_scan(ecnt[:, 2], ones_f[:, 0:E], ecnt[:, 1], 0.0, ALU.mult, ALU.add))
            link(dve.tensor_tensor(ecnt[:, 3], ecnt[:, 2], ecnt[:, 1], ALU.subtract))
            link(dve.scalar_tensor_tensor(out=ecnt[:, 3], in0=ecnt[:, 3], scalar=float(P), in1=edge[:, 0:E],
                                          op0=ALU.mult, op1=ALU.subtract))
            link(dve.tensor_tensor(cum, cum, tot, ALU.subtract))
            link(dve.tensor_tensor(cum, cum, ecnt[:, 3].unsqueeze(2).to_broadcast([P, E, NT]), ALU.add))
            link(dve.tensor_tensor(pos, ps[:, 7, 0:NT * E].rearrange("p (t e) -> p t e", e=E),
                                   cum.rearrange("p e t -> p t e"), ALU.add))
            for k in range(TOP):
                ins = dve.tensor_tensor(picked[:, k], sel[:, k], pos, ALU.mult)
            link(ins)
            link(dve.tensor_reduce(slot[:, 0], picked.rearrange("p k t e -> p (k t) e"), AX.X, ALU.add))
            link(dve.tensor_copy(slot_i[:, 0], slot[:, 0]))
            dve.tensor_scalar(slot_i[:, 1], slot_i[:, 0], 7, None, ALU.arith_shift_right)
            link(dve.tensor_scalar(slot_i[:, 2], slot_i[:, 0], P - 1, None, ALU.bitwise_and))
            link(dve.tensor_copy(slot[:, 1:3], slot_i[:, 1:3]))
            tile_of = slot[:, 1].rearrange("p (k t) -> p k t", k=TOP)
            for k in range(TOP):
                ins = dve.tensor_tensor(at_tile[:, k], tile_no[:].unsqueeze(1).to_broadcast([P, NT, TILES]),
                                        tile_of[:, k].unsqueeze(2).to_broadcast([P, NT, TILES]), ALU.is_equal)
                ins.then_inc(at_tile_made, 1)
            for n in range(PAIRS):
                ins = dve.tensor_scalar(at_lane[:, n], lane_no[:], slot[:, 2, n:n + 1], None, ALU.is_equal)
                if n % 8 == 7:
                    ins.then_inc(coded_made, 1)
            dve.wait_ge(coded_out, 1)
            link(dve.tensor_copy(code.rearrange("p c a -> p (c a)"), ps[:, 7, 256:256 + 2 * TILES]))
            dve.scalar_tensor_tensor(out=dstf[:, 0], in0=code[:, 0], scalar=0.0, in1=unused_row[:], op0=ALU.is_equal, op1=ALU.mult)
            link(dve.scalar_tensor_tensor(out=dstf[:, 1], in0=code[:, 0], scalar=float(NT), in1=code[:, 1],
                                          op0=ALU.mult, op1=ALU.add))
            link(dve.scalar_tensor_tensor(out=pair[:], in0=dstf[:, 1], scalar=float(-NT), in1=dstf[:, 0],
                                          op0=ALU.add, op1=ALU.add))
            dve.tensor_scalar(src[:], pair[:], B * S - 1, None, ALU.bitwise_and).then_inc(index_made, 1)
            link(dve.tensor_scalar(slot_i2, pair[:], 12, 11, ALU.arith_shift_right, ALU.arith_shift_left))
            dve.wait_ge(index_made, 1)
            dve.tensor_tensor(dst[:], src[:], slot_i2, ALU.add).then_inc(dst_made, 1)

            dve.tensor_tensor(ecmp, tile_no[0:1].unsqueeze(2).to_broadcast([1, TILES, E]),
                              ecnt[0:1, 2].unsqueeze(1).to_broadcast([1, TILES, E]), ALU.is_ge).then_inc(dve_step, 1)
            steps[0] += 1
            dve.wait_ge(dve_step, steps[0])
            link(dve.tensor_reduce(etab_f, ecmp, AX.X, ALU.add))
            dve.tensor_copy(etab[:, TILES:TILES + 1], ecnt[0:1, 2, E - 1:E])
            dve.tensor_scalar(etab[:, 0:TILES], etab_f, float(E - 1), float(2 * CHUNK), ALU.min, ALU.mult).then_inc(etab_made, 1)
            link(dve.tensor_copy(smx[:, 0], top[:, :, 0]))
            dve.tensor_tensor(top[:], top[:], smx[:, 0].unsqueeze(2).to_broadcast([P, NT, E]), ALU.subtract).then_inc(w_centred, 1)
            dve.wait_ge(w_exped, 1)
            link(dve.tensor_reduce(smx[:, 1], top[:], AX.X, ALU.add))
            link(dve.reciprocal(smx[:, 0], smx[:, 1]))
            link(dve.tensor_scalar(smx[:, 1], smx[:, 0], tg[:, 1:2], 1.0 / (W_SCALE * H_SCALE), ALU.mult, ALU.mult))
            for k in range(TOP):
                ins = dve.tensor_tensor(wts[:, k], top[:, :, k], smx[:, 1], ALU.mult)
            ins.then_inc(weights_made, 1)

            def prepare(j, s):
                dve.wait_ge(uT_ready, j + 1)
                for k in range(KD):
                    ins = dve.tensor_scalar(xf[:, k], ps[:, 6, k * P:(k + 1) * P], gb16[:, k, 0:1], gb16[:, k, 1:2],
                                            ALU.mult, ALU.add)
                ins.then_inc(xf_made, 1)
                dve.wait_ge(xf_made, j + 1)
                dve.tensor_copy(xh[:, s], xf).then_inc(xh_made, 1)
                dve.wait_ge(xh_made, j + 1)
                dve.tensor_tensor(xl[:, s], xf, xh[:, s], ALU.subtract).then_inc(x_ready, 1)

            def evacuate(j, s, turn):
                dve.wait_ge(y_ready, j + 1)
                if not isinstance(turn, int) or turn > 0:
                    dve.wait_ge(scattered[s], turn * 16)
                dve.wait_ge(weighed[s], turn * 16 + 16)
                dve.tensor_scalar(ys[:, s], ps[:, 7, 0:D], slot_w[:, s:s + 1], None, ALU.mult).then_inc(y_out, 1)

            def lower_hidden(j):
                for half in range(2):
                    part = slice(512 * half, 512 * half + 512)
                    dve.wait_ge(hh_made, j * 2 + (half + 1))
                    dve.scalar_tensor_tensor(out=hl[:, part], in0=ps[:, 2 + half], scalar=H_SCALE, in1=hh[:, part],
                                             op0=ALU.mult, op1=ALU.subtract).then_inc(split_done, 1)

            def step(j, s, turn):
                if not isinstance(j, int) or j > 1:
                    evacuate(j - 2, (s + 1) % 3, turn - (s < 2))
                if not isinstance(j, int) or j > 0:
                    lower_hidden(j - 1)
                prepare(j + 1, (s + 1) % 3)
                for n in late(LATE_LOWER, j):
                    lower(n)

            prepare(0, 0)

            def finish(n):
                evacuate(n - 2, (n - 2) % 3, (n - 2) // 3)
                lower_hidden(n - 1)
                evacuate(n - 1, (n - 1) % 3, (n - 1) // 3)

            run_tiles(dve, mybir.EngineType.DVE, step, finish)

        @block.tensor
        def _(pe):
            def keep_warm(times, bank):
                for _ in range(times):
                    pe.matmul(ps[:, bank].rearrange("p (n q) -> p n q", n=4), ones_b[:],
                              ones_b[:].unsqueeze(1).to_broadcast([P, 4, P]), start=True, stop=True)

            pe.wait_ge(warm_made, 1)
            keep_warm(WARM[0], 2)
            pe.wait_ge(ident_made, 1)
            pe.wait_ge(rows_in, 16 * N_ROWS)
            for k in range(KD):
                pe.transpose(ps[:, 7, 12 * k:12 * k + 12], rows[0:12, k * P:(k + 1) * P], ident[0:12, 0:12])
            for k in range(KD):
                for b in range(B):
                    n = (k * B + b) * C
                    ins = pe.transpose(ps[:, 6, n:n + C], ctx_sb[0:C, b, k * P:(k + 1) * P], ident[0:C, 0:C])
            ins.then_inc(setup_pe, 1)
            pe.wait_ge(wq_in, 16)
            for m in range(KD):
                for k in range(KD):
                    ins = pe.transpose(ps[:, 4, (m * KD + k) * P:(m * KD + k + 1) * P], wq_sb[:, k, m * P:(m + 1) * P], ident[:])
            ins.then_inc(setup_pe, 1)
            pe.wait_ge(wk_in, 16)
            pe.wait_ge(setup_copied, 2)
            for m in range(KD):
                for k in range(KD):
                    ins = pe.matmul(ps[:, 5, m * B * C:(m + 1) * B * C], wk_sb[:, k, m * P:(m + 1) * P], ctxT[:, k],
                                    start=(k == 0), stop=(k == KD - 1))
            ins.then_inc(setup_pe, 1)

            def turn_x(g):
                pe.wait_ge(xn_made, g + 1)
                for i in range(G):
                    for k in range(KD):
                        ins = pe.transpose(ps[:, k, i * P:(i + 1) * P], xn[g % 2][:, i, k * P:(k + 1) * P], ident[:])
                ins.then_inc(x_turned, 1)

            def score(g):
                if g >= 1:
                    pe.wait_ge(centred, g)
                b = g // 2
                pe.matmul(ps[:, 2, 0:G * C].rearrange("p (i c) -> p i c", i=G), ones_f[:],
                          s_bias[:, b * C:(b + 1) * C].unsqueeze(1).to_broadcast([P, G, C]), start=True, stop=False)
                pe.wait_ge(xT_made, KD * (g + 1))
                for i in range(G):
                    for k in range(KD):
                        ins = pe.matmul(ps[:, 2, i * C:(i + 1) * C], xT[:, k, i * P:(i + 1) * P],
                                        gk[:, k, b * C:(b + 1) * C], start=False, stop=(i == G - 1 and k == KD - 1))
                ins.then_inc(scored, 1)

            def turn_p(g):
                pe.wait_ge(exped, g + 1)
                for i in range(G):
                    ins = pe.transpose(ps[0:C, 3, i * P:(i + 1) * P], pr[:, g % 2, i], ident[:])
                ins.then_inc(p_turned, 1)

            def attend(g):
                pe.wait_ge(pT_made, g + 1)
                if g >= 1:
                    pe.wait_ge(x2_made, g)
                for i in range(G):
                    ins = pe.matmul(ps[:, 4 + i // 2, D * (i % 2):D * (i % 2) + D], pT[0:C, i * P:(i + 1) * P],
                                    v_sb[0:C, (g // 2) * D:(g // 2 + 1) * D], start=True, stop=True)
                ins.then_inc(attended, 1)

            def turn_u(g):
                pe.wait_ge(u_made, g + 1)
                if g >= 1:
                    pe.wait_ge(logits_read, g)
                for k in range(KD):
                    for i in range(G):
                        ins = pe.transpose(ps[:, 6 + k, i * P:(i + 1) * P], ub[:, g % 2, i, k * P:(k + 1) * P], ident[:])
                ins.then_inc(u_turned, 1)

            def route(g):
                keep_warm(WARM[6], 0)
                pe.wait_ge(uT_made, KD * (g + 1))
                o = ps[:, 7, 0:G * E]
                pe.matmul(o.rearrange("p (i e) -> p i e", i=G), ones_f[:], r_bias.unsqueeze(1).to_broadcast([P, G, E]),
                          start=True, stop=False)
                for i in range(G):
                    for k in range(KD):
                        ins = pe.matmul(o[:, i * E:(i + 1) * E], uT[:, k, i * P:(i + 1) * P], rg[:, k],
                                        start=False, stop=(i == G - 1 and k == KD - 1))
                ins.then_inc(logits_done, 1)

            turn_x(0)
            pe.wait_ge(setup_copied, 5)
            for k in range(KD):
                for m in range(KD):
                    pe.matmul(ps[:, 4, k * B * C:(k + 1) * B * C], wqT[:, m, k * P:(k + 1) * P], kT[:, m],
                              start=(m == 0), stop=(m == KD - 1))
            for m in range(KD):
                pe.matmul(ps[0:1, 7, 32:32 + B * C], cols[:, m, 0:1], kT[:, m], start=(m == 0), stop=(m == KD - 1))
            for k in range(KD):
                ins = pe.matmul(ps[0:1, 7, 200:208], cols[:, k, 3:4], cols[:, k, 4:12], start=(k == 0), stop=(k == KD - 1))
            ins.then_inc(setup_pe, 1)
            pe.wait_ge(const_made, 2)
            pe.wait_ge(setup_copied, 7)
            score(0)
            pe.wait_ge(wv_in, 16)
            pe.wait_ge(vectors_in, 16 * N_VECTORS)
            for b in range(B):
                for k in range(KD):
                    pe.matmul(ps[0:C, 3, b * D:(b + 1) * D], ctxT[:, k, b * C:(b + 1) * C], wv_sb[:, k],
                              start=(k == 0), stop=False)
                pe.matmul(ps[0:C, 3, b * D:(b + 1) * D], ones_f[:, 0:C], bv_sb, start=False, stop=True)
            pe.matmul(ps[:, 5, 400:402], ones_f[:], g_sb, start=True, stop=True).then_inc(setup_pe, 1)
            pe.wait_ge(setup_copied, 12)
            pe.wait_ge(gates_made, 1)
            for t in range(NG):
                keep_warm(WARM[1][t], 0)
                turn_p(t)
                if t + 1 < NG:
                    turn_x(t + 1)
                keep_warm(WARM[4], 2)
                attend(t)
                if t + 1 < NG:
                    score(t + 1)
                if t >= 1:
                    turn_u(t - 1)
                    route(t - 1)
            keep_warm(WARM[2], 0)
            turn_u(NG - 1)
            route(NG - 1)

            pe.wait_ge(ranked, NG)
            pe.matmul(ps[:, 7, 0:NT * E], before[:], sel_sum[:], start=True, stop=True)
            pe.matmul(ps[:, 7, NT * E:2 * NT * E], ones_b[:], sel_sum[:], start=True, stop=True).then_inc(counted, 1)
            for n in range(PAIRS):
                if n % 8 == 0:
                    pe.wait_ge(coded_made, n // 8 + 1)
                if n % NT == 0:
                    pe.wait_ge(codes_made, n // NT + 1)
                    pe.wait_ge(lanes_made, n // NT + 1)
                ins = pe.matmul(ps[:, 7, 256:256 + 2 * TILES], at_lane[:, n],
                                coded[:, n // NT, n % NT].rearrange("p c a -> p (c a)"),
                                start=(n == 0), stop=(n == PAIRS - 1))
            ins.then_inc(coded_out, 1)

            def turn_rows(j, s, turn):
                pe.wait_ge(gathered[s], (turn + 1) * 16)
                if not isinstance(j, int) or j > 0:
                    pe.wait_ge(x_ready, j)
                for k in range(KD):
                    ins = pe.transpose(ps[:, 6, k * P:(k + 1) * P], ug[:, s, k * P:(k + 1) * P], ident[:])
                ins.then_inc(uT_ready, 1)

            def hidden(j, s, at):
                pe.wait_ge(x_ready, j + 1)
                if j_of(j) is not None:
                    pe.wait_ge(w_lo_made, 2 * min(j_of(j), E - 1) + 2)
                for half in range(2):
                    o = ps[:, half]
                    for k in range(KD):
                        part = bass.ds(at + (k * H + half * 512), 512)
                        pe.matmul(o, xh[:, s, k], w_hi[:, part], start=(k == 0), stop=False)
                        pe.matmul(o, xh[:, s, k], w_lo[:, part], start=False, stop=False)
                        ins = pe.matmul(o, xl[:, s, k], w_hi[:, part], start=False, stop=(k == KD - 1))
                    ins.then_inc(h_ready, 1)

            def turn_hidden(j):
                for c in range(HC):
                    if c % 4 == 0:
                        pe.wait_ge(silu_done, j * 2 + (c // 4 + 1))
                    ins = pe.transpose(ps[:, 2 + c // 4, (c % 4) * P:(c % 4 + 1) * P], hs[:, c * P:(c + 1) * P], ident[:])
                    if c % 4 == 3:
                        ins.then_inc(hT_ready, 1)

            def back(j, at):
                pe.wait_ge(split_done, j * 2 + 2)
                if not isinstance(j, int) or j > 0:
                    pe.wait_ge(y_out, j)
                o = ps[:, 7, 0:D]
                for c in range(HC):
                    part = bass.ds(at + (CHUNK + c * D), D)
                    hi, lo = hh[:, c * P:(c + 1) * P], hl[:, c * P:(c + 1) * P]
                    pe.matmul(o, hi, w_hi[:, part], start=(c == 0), stop=False)
                    pe.matmul(o, hi, w_lo[:, part], start=False, stop=False)
                    ins = pe.matmul(o, lo, w_hi[:, part], start=False, stop=(c == HC - 1))
                ins.then_inc(y_ready, 1)

            def j_of(j):
                return j if isinstance(j, int) else None

            def place(j):
                return nc.values_load(etab[0:1, bass.ds(j, 1)] if not isinstance(j, int) else etab[0:1, j:j + 1],
                                      engines=(mybir.EngineType.PE,), min_val=0, max_val=(E - 1) * 2 * CHUNK,
                                      skip_runtime_bounds_check_because="the table's entries are clamped to the experts")

            known = {}

            def step(j, s, turn):
                turn_rows(j + 1, (s + 1) % 3, turn + (s == 2))
                if j_of(j) != 0:
                    turn_hidden(j - 1)
                if j_of(j) is None and s == PEELED % 3:
                    pe.wait_ge(w_lo_made, NW)
                if (j_of(j) is None and s == PEELED % 3) or (j_of(j) is not None and j > PEELED):
                    known["last"] = place(j - 1)
                at = place(j)
                hidden(j, s, at)
                if j_of(j) != 0:
                    back(j - 1, known["last"])
                known["last"] = at

            keep_warm(WARM[3], 0)
            pe.wait_ge(etab_made, 1)
            turn_rows(0, 0, 0)
            keep_warm(WARM[5], 0)

            def finish(n):
                turn_hidden(n - 1)
                back(n - 1, place(n - 1))

            run_tiles(pe, mybir.EngineType.PE, step, finish)


_INS = ["x", "ctx_1024", "g_xattn", "g_ffn", "L0_xattn_Wq", "L0_xattn_bq", "L0_xattn_Wk", "L0_xattn_bk",
        "L0_xattn_Wv", "L0_xattn_bv", "L0_ffn_gamma", "L0_ffn_beta", "L0_ffn_router_w", "L0_ffn_W1", "L0_ffn_W2"]


def kernel(**inputs):
    import numpy as _np
    import concourse.bacc as _bacc
    from concourse import mybir as _mybir
    from concourse.bass_utils import run_bass_kernel_spmd as _run

    nc = _bacc.Bacc("TRN2", target_bir_lowering=False, num_devices=1)
    arrays, args = {}, []
    for name in _INS:
        a = _np.ascontiguousarray(inputs[name])
        arrays[f"in_{name}"] = a
        args.append(nc.dram_tensor(f"in_{name}", a.shape, _mybir.dt.from_np(a.dtype), kind="ExternalInput").ap())
    out = nc.dram_tensor("out_0", (B, S, D), F32, kind="ExternalOutput").ap()
    gated_attention_moe(nc, *args, out)
    r = _run(nc, [arrays], core_ids=[0])
    return r.results[0]["out_0"]
```
